# Optimizing a Trainium2 kernel written in Bass

```python
import numpy as np
import jax
import jax.numpy as jnp

def _softmax(x, axis=-1):
    return jax.nn.softmax(x, axis=axis)

def _gelu(x):
    return jax.nn.gelu(x, approximate=True)

def _silu(x):
    return jax.nn.silu(x)

def _sigmoid(x):
    return jax.nn.sigmoid(x)

def _layernorm(x, axis=-1, eps=1e-05):
    m = jnp.mean(x, axis=axis, keepdims=True)
    v = jnp.var(x, axis=axis, keepdims=True)
    return (x - m) / jnp.sqrt(v + eps)

def _scatter_add(tgt, idx, src, axis=0):
    return tgt.at[idx].add(src)

def _segment_sum(src, seg, n):
    return jax.ops.segment_sum(src, seg, n)
kernel_name = 'mk_gps_d1_gnn_r8_47cd07'

def setup_inputs(seed: int=0):
    np.random.seed(seed)
    _w = jnp.asarray

    def _rec_inputs():
        import jax
        import jax.numpy as jnp
        _gk = jax.random.key(seed)
        x = -0.0003713 + 1 * jax.random.normal(jax.random.fold_in(_gk, 1), (6250, 256), jnp.float32)
        _s = jax.random.randint(jax.random.fold_in(_gk, 2), (50000,), 0, 6250, jnp.int32)
        _d = jax.random.randint(jax.random.fold_in(_gk, 3), (50000,), 0, 6250, jnp.int32)
        _loop = jnp.arange(6250, dtype=jnp.int32)
        src = jnp.concatenate([_s, _d, _loop])
        dst = jnp.concatenate([_d, _s, _loop])
        _o = jnp.argsort(dst, stable=True)
        src = src[_o]
        dst = dst[_o]
        edge_attr_256 = -8.16379e-05 + 0.999858 * jax.random.normal(jax.random.fold_in(_gk, 12), (106250, 256), jnp.float32)
        return (x, src, dst, edge_attr_256)
    x, src, dst, edge_attr_256 = _rec_inputs()

    def _L0_gnn_setup():
        import jax, jax.numpy as jnp
        import numpy as np
        N_SRC = 6250
        N_DST = 6250
        E = 50000
        D_IN = 256
        D_OUT = 256
        key = jax.random.key(seed)
        k1, k2, k3, k4, k5 = jax.random.split(key, 5)
        src_feats = jax.random.normal(k1, (N_SRC, D_IN), dtype=jnp.float32)
        edge_feats = jax.random.normal(k2, (E, D_IN), dtype=jnp.float32)
        src_idx = jax.random.randint(k3, (E,), 0, N_SRC, dtype=jnp.int32)
        dst_idx = jax.random.randint(k4, (E,), 0, N_DST, dtype=jnp.int32)
        fan_in, fan_out = (2 * D_IN, D_OUT)
        bound = np.sqrt(6.0 / (fan_in + fan_out))
        weights = jax.random.uniform(k5, (2 * D_IN, D_OUT), dtype=jnp.float32, minval=-bound, maxval=bound)
        h_bias = jnp.zeros((D_OUT,), dtype=jnp.float32)
        return {'src_feats': src_feats, 'edge_feats': edge_feats, 'src_idx': src_idx, 'dst_idx': dst_idx, 'weights': weights, 'h_bias': h_bias, 'num_dst': N_DST}
    _L0_gnn_all = _L0_gnn_setup()
    _L0_gnn_in = {k: v for k, v in _L0_gnn_all.items() if k in ('weights', 'h_bias')}
    del _L0_gnn_all

    def _L0_mix_setup():
        import jax, jax.numpy as jnp
        import numpy as np
        MIDC = 256
        HEADS = 8
        HEADC = MIDC // HEADS
        EPS = 1e-05

        def _ln(x, gamma, beta):
            mu = jnp.mean(x, axis=-1, keepdims=True)
            var = jnp.var(x, axis=-1, keepdims=True)
            return (x - mu) * jax.lax.rsqrt(var + EPS) * gamma + beta
        key = jax.random.key(seed)
        ks = jax.random.split(key, 8)
        B, HW, C = (8, 512, MIDC)
        s = 1.0 / np.sqrt(C)
        return {'x': jax.random.normal(ks[0], (B, HW, C), jnp.float32), 'w_qkv': jax.random.normal(ks[1], (C, 3 * C), jnp.float32) * s, 'b_qkv': jnp.zeros((3 * C,), jnp.float32), 'kln_g': jnp.ones((HEADC,), jnp.float32), 'kln_b': jnp.zeros((HEADC,), jnp.float32), 'vln_g': jnp.ones((HEADC,), jnp.float32), 'vln_b': jnp.zeros((HEADC,), jnp.float32), 'w1': jax.random.normal(ks[2], (C, C), jnp.float32) * s, 'b1': jnp.zeros((C,), jnp.float32), 'w2': jax.random.normal(ks[3], (C, C), jnp.float32) * s, 'b2': jnp.zeros((C,), jnp.float32)}
    _L0_mix_all = _L0_mix_setup()
    _L0_mix_in = {k: v for k, v in _L0_mix_all.items() if k in ('w_qkv', 'b_qkv', 'kln_g', 'kln_b', 'vln_g', 'vln_b', 'w1', 'b1', 'w2', 'b2')}
    del _L0_mix_all

    def _L0_ffn_setup():
        import math
        import jax, jax.numpy as jnp
        import numpy as np
        CAPACITY_FACTOR = 1.25
        TOP_K = 2
        LN_EPS = 1e-05

        def _layer_norm(x, gamma, beta):
            mu = jnp.mean(x, axis=-1, keepdims=True)
            var = jnp.var(x, axis=-1, keepdims=True)
            return (x - mu) * jax.lax.rsqrt(var + LN_EPS) * gamma + beta
        key = jax.random.key(seed)
        ks = jax.random.split(key, 4)
        B, S, D, F, E = (8, 512, 256, 512, 8)
        x = jax.random.normal(ks[0], (B, S, D), dtype=jnp.float32)
        Wr = jax.random.normal(ks[1], (D, E), dtype=jnp.float32) / np.sqrt(D)
        br = jnp.zeros((E,), jnp.float32)
        W1 = jax.random.normal(ks[2], (E, D, F), dtype=jnp.float32) / np.sqrt(D)
        b1 = jnp.zeros((E, F), jnp.float32)
        W2 = jax.random.normal(ks[3], (E, F, D), dtype=jnp.float32) / np.sqrt(F)
        b2 = jnp.zeros((E, D), jnp.float32)
        gamma = jnp.ones((D,), jnp.float32)
        beta = jnp.zeros((D,), jnp.float32)
        return {'x': x, 'Wr': Wr, 'br': br, 'W1': W1, 'b1': b1, 'W2': W2, 'b2': b2, 'gamma': gamma, 'beta': beta}
    _L0_ffn_all = _L0_ffn_setup()
    _L0_ffn_in = {k: v for k, v in _L0_ffn_all.items() if k in ('Wr', 'br', 'W1', 'b1', 'W2', 'b2', 'gamma', 'beta')}
    del _L0_ffn_all
    return {'x': x, 'src': src, 'dst': dst, 'edge_attr_256': edge_attr_256, 'L0_gnn_weights': _L0_gnn_in['weights'], 'L0_gnn_h_bias': _L0_gnn_in['h_bias'], 'L0_mix_w_qkv': _L0_mix_in['w_qkv'], 'L0_mix_b_qkv': _L0_mix_in['b_qkv'], 'L0_mix_kln_g': _L0_mix_in['kln_g'], 'L0_mix_kln_b': _L0_mix_in['kln_b'], 'L0_mix_vln_g': _L0_mix_in['vln_g'], 'L0_mix_vln_b': _L0_mix_in['vln_b'], 'L0_mix_w1': _L0_mix_in['w1'], 'L0_mix_b1': _L0_mix_in['b1'], 'L0_mix_w2': _L0_mix_in['w2'], 'L0_mix_b2': _L0_mix_in['b2'], 'L0_ffn_Wr': _L0_ffn_in['Wr'], 'L0_ffn_br': _L0_ffn_in['br'], 'L0_ffn_W1': _L0_ffn_in['W1'], 'L0_ffn_b1': _L0_ffn_in['b1'], 'L0_ffn_W2': _L0_ffn_in['W2'], 'L0_ffn_b2': _L0_ffn_in['b2'], 'L0_ffn_gamma': _L0_ffn_in['gamma'], 'L0_ffn_beta': _L0_ffn_in['beta']}

def reference(x, src, dst, edge_attr_256, L0_gnn_weights, L0_gnn_h_bias, L0_mix_w_qkv, L0_mix_b_qkv, L0_mix_kln_g, L0_mix_kln_b, L0_mix_vln_g, L0_mix_vln_b, L0_mix_w1, L0_mix_b1, L0_mix_w2, L0_mix_b2, L0_ffn_Wr, L0_ffn_br, L0_ffn_W1, L0_ffn_b1, L0_ffn_W2, L0_ffn_b2, L0_ffn_gamma, L0_ffn_beta):
    import jax
    import jax.numpy as jnp

    def _L0_gnn_ref(src_feats, edge_feats, src_idx, dst_idx, weights, h_bias, num_dst):
        import jax, jax.numpy as jnp
        import numpy as np
        N_SRC = 6250
        N_DST = 6250
        E = 50000
        D_IN = 256
        D_OUT = 256
        d = src_feats.shape[1]
        m = src_feats[src_idx] @ weights[:d] + edge_feats @ weights[d:]
        deg = jax.ops.segment_sum(jnp.ones((m.shape[0],), jnp.float32), dst_idx, num_segments=num_dst)
        norm = jnp.where(deg > 0, jax.lax.rsqrt(jnp.maximum(deg, 1.0)), 0.0)
        h = jax.ops.segment_sum(m * norm[dst_idx][:, None], dst_idx, num_segments=num_dst)
        return h + h_bias

    def _L0_mix_ref(x, w_qkv, b_qkv, kln_g, kln_b, vln_g, vln_b, w1, b1, w2, b2):
        import jax, jax.numpy as jnp
        import numpy as np
        MIDC = 256
        HEADS = 8
        HEADC = MIDC // HEADS
        EPS = 1e-05

        def _ln(x, gamma, beta):
            mu = jnp.mean(x, axis=-1, keepdims=True)
            var = jnp.var(x, axis=-1, keepdims=True)
            return (x - mu) * jax.lax.rsqrt(var + EPS) * gamma + beta
        B, HW, C = x.shape
        bias = x
        qkv = (x @ w_qkv + b_qkv).reshape(B, HW, HEADS, 3 * HEADC)
        qkv = qkv.transpose(0, 2, 1, 3)
        q, k, v = jnp.split(qkv, 3, axis=-1)
        k = _ln(k, kln_g, kln_b)
        v = _ln(v, vln_g, vln_b)
        kv = jnp.einsum('bhnd,bhne->bhde', k, v) / HW
        out = jnp.einsum('bhnd,bhde->bhne', q, kv)
        out = out.transpose(0, 2, 1, 3).reshape(B, HW, C)
        ret = out + bias
        h = jax.nn.gelu(ret @ w1 + b1, approximate=False)
        return h @ w2 + b2 + bias

    def _L0_ffn_ref(x, Wr, br, W1, b1, W2, b2, gamma, beta):
        import math
        import jax, jax.numpy as jnp
        import numpy as np
        CAPACITY_FACTOR = 1.25
        TOP_K = 2
        LN_EPS = 1e-05

        def _layer_norm(x, gamma, beta):
            mu = jnp.mean(x, axis=-1, keepdims=True)
            var = jnp.var(x, axis=-1, keepdims=True)
            return (x - mu) * jax.lax.rsqrt(var + LN_EPS) * gamma + beta
        B, S, D = x.shape
        E = Wr.shape[1]
        N = B * S
        K = TOP_K
        logits = jnp.mean(x, axis=1) @ Wr + br
        routing_weights = jax.nn.softmax(logits, axis=-1)
        capacity = float(math.ceil(N * CAPACITY_FACTOR / E))
        expected_loads = routing_weights.sum(axis=0) * (N / B)
        scale = jnp.where(expected_loads > capacity, capacity / expected_loads, 1.0)
        routing_weights = jax.nn.softmax(routing_weights * scale, axis=-1)
        rw_tok = jnp.broadcast_to(routing_weights[:, None, :], (B, S, E)).reshape(N, E)
        top_w, top_i = jax.lax.top_k(rw_tok, K)
        top_w = jax.nn.softmax(top_w, axis=-1)
        xf = x.reshape(N, D)
        h = jax.nn.gelu(jnp.einsum('nd,edf->enf', xf, W1) + b1[:, None, :], approximate=False)
        y = jnp.einsum('enf,efd->end', h, W2) + b2[:, None, :]
        w_dense = jnp.zeros((N, E), x.dtype).at[jnp.arange(N)[:, None], top_i].add(top_w)
        out = jnp.einsum('ne,end->nd', w_dense, y).reshape(B, S, D)
        out = _layer_norm(out + x, gamma, beta)
        return out
    xn = _layernorm(x, axis=-1)
    x = x + _L0_gnn_ref(xn, edge_attr_256, src, dst, L0_gnn_weights, L0_gnn_h_bias, 6250) + _L0_mix_ref(xn[None], L0_mix_w_qkv, L0_mix_b_qkv, L0_mix_kln_g, L0_mix_kln_b, L0_mix_vln_g, L0_mix_vln_b, L0_mix_w1, L0_mix_b1, L0_mix_w2, L0_mix_b2)[0]
    x = x + _L0_ffn_ref(_layernorm(x, axis=-1)[None], L0_ffn_Wr, L0_ffn_br, L0_ffn_W1, L0_ffn_b1, L0_ffn_W2, L0_ffn_b2, L0_ffn_gamma, L0_ffn_beta)[0]
    return x

_drawn_inputs = setup_inputs


def setup_inputs(seed=0):
    import zlib

    import numpy as np

    out = dict(_drawn_inputs(seed))
    spreads = {'L0_gnn_h_bias': (0.0, 0.1),
     'L0_mix_b_qkv': (0.0, 0.297),
     'L0_mix_kln_g': (1.0, 0.6),
     'L0_mix_kln_b': (0.0, 0.502),
     'L0_mix_vln_g': (1.0, 0.6),
     'L0_mix_vln_b': (0.0, 0.452),
     'L0_mix_b1': (0.0, 0.293),
     'L0_mix_b2': (0.0, 0.1),
     'L0_ffn_br': (0.0, 0.1),
     'L0_ffn_b1': (0.0, 0.634),
     'L0_ffn_b2': (0.0, 0.427),
     'L0_ffn_gamma': (1.0, 0.2),
     'L0_ffn_beta': (0.0, 0.271)}
    factors = {}
    for name, (base, spread) in spreads.items():
        noise = np.random.default_rng([zlib.crc32(name.encode()), seed]).standard_normal(out[name].shape)
        drawn = base * np.exp(spread * noise) if base else spread * noise
        out[name] = jnp.asarray(drawn.astype(out[name].dtype))
    for name, factor in factors.items():
        out[name] = (out[name] * factor).astype(out[name].dtype)
    return out
```

```python
from contextlib import ExitStack

import concourse.bass as bass
from concourse import mybir

ALU = mybir.AluOpType
ACT = mybir.ActivationFunctionType
AX = mybir.AxisListType.X
F32 = mybir.dt.float32
F32R = mybir.dt.float32r
F16 = mybir.dt.float16
I32 = mybir.dt.int32
U32 = mybir.dt.uint32
ds = bass.ds

P = 128
N = 6250
D = 256
E = 106250
KC = D // P
TN = 125
NT = N // TN
CN = 2 * TN
NC = NT // 2
CW = 256
GT = 10
HT = GT // 2
GE = P * GT
NG = -(-E // GE)
LAST = E - GE
W = 128
PASSES = -(-N // W)
NPAD = PASSES * W + W
HEADS = 8
HC = D // HEADS
GR = 2 * HEADS
EX = 8
F = 512
FC = 2 * F // P
EPS = 1e-5
CAPACITY = float(-(-N * 5 // (4 * EX)))
BLK = 10
GAP = 12000
MASKED = 1.0e6


def fin(it, back=0):
    return it + 3 - back


def wait_past(eng, semaphore, value):
    if not (isinstance(value, int) and value <= 0):
        eng.wait_ge(semaphore, value)


def gps_layer(nc, x, src_l, dst_l, edges, wgnn, hbias, w_qkv, wq_t, b_qkv, bq_l, kln_g, kln_b, vln_g, vln_b,
              w1, b1_l, w2, b2, wr, br, fw1, fb1_l, fw2, fb2, gamma, beta, out):
    ctx = ExitStack()
    with ctx:
        def alloc(stack):
            return lambda name, shape, dt=F32: stack.enter_context(nc.sbuf_tensor(name, shape, dt))

        def sem(name):
            return ctx.enter_context(nc.semaphore(name))

        table = nc.dram_tensor("xn_table", [N, 2 * D], F16, kind="Internal").ap()
        base_d = nc.dram_tensor("base_rows", [CN + N, D], F32, kind="Internal").ap()
        deg_d = nc.dram_tensor("deg_row", [1, N], F32, kind="Internal").ap()

        sb = alloc(ctx)
        ident = sb("ident", [P, P])
        ones = sb("ones", [P, P])
        r1 = sb("r1", [TN, NT])
        nmr1 = sb("nmr1", [TN, NT])
        r2 = sb("r2", [TN, NT])
        nmr2 = sb("nmr2", [TN, NT])
        norm = sb("norm", [TN, NT])
        ok_i = sb("ok_i", [1, 1], I32)

        sums = ExitStack()
        sbs = alloc(sums)
        acc_y = sbs("acc_y", [P, KC, NPAD])
        deg_row = sbs("deg_row_sb", [1, NPAD])
        edge_phase = ExitStack()
        sbe = alloc(edge_phase)
        gring = sbe("gring", [P, 2 * GT, 2 * D], F16)
        e32 = sbe("e32", [P, GT, D])
        e_hi = sbe("e_hi", [P, GT, D], F32R)
        e_lo = sbe("e_lo", [P, GT, D], F32R)
        s32 = sbe("s32", [P, GT, W], F32R)
        s16 = sbe("s16", [P, GT, W], F16)
        ones16 = sbe("ones16", [P, 1], F16)
        iota = sbe("iota", [P, W])
        iota_i = sbe("iota_i", [P, W], I32)
        rel = sbe("rel", [P, NG * GT])
        src_sb = sbe("src_sb", [P, NG * GT], I32)
        idx = sbe("idx", [P, 2 * GT], I32)
        gmin = sbe("gmin", [P, NG])
        bcol = sbe("bcol", [NG, 1])
        bcol_w = sbe("bcol_w", [NG, P])
        bwide = sbe("bwide", [P, NG])
        brow = sbe("brow", [1, NG + 1], I32)
        okc = sbe("okc", [P, 4])
        fl = sbe("fl", [P, 2 * D])
        fl_t = sbe("fl_t", [P, 4, W])
        wg = sbe("wg", [P, 4, D])
        wkv_hi = sbe("wkv_hi", [P, KC, 2 * D], F32R)
        wkv_lo = sbe("wkv_lo", [P, KC, 2 * D], F32R)
        bkv = sbe("bkv", [TN, 2 * D])
        lns = sbe("lns", [TN, 4, HC])
        m_hi = sbe("m_hi", [P, KC, D], F32R)
        m_lo = sbe("m_lo", [P, KC, D], F32R)
        w2_hi = sbe("w2_hi", [P, KC, D], F32R)
        w2_lo = sbe("w2_lo", [P, KC, D], F32R)
        wq_sb = sbe("wq_sb", [P, KC, D])
        w1_sb = sbe("w1_sb", [P, KC, D])
        p_sb = sbe("p_sb", [P, KC, D])
        bq = sbe("bq", [P, KC])
        b1c = sbe("b1c", [P, KC])
        bm = sbe("bm", [P, KC])
        brows = sbe("brows", [TN, D])
        hrows = sbe("hrows", [TN, D])
        block_mask = sbe("block_mask", [P, P])
        kv_t = sbe("kv_t", [P, KC, P])
        xch = sbe("xch", [TN, 2, 2, D])
        xnc = sbe("xnc", [TN, 2, D])
        xt_hi = sbe("xt_hi", [P, KC, CW], F32R)
        xt_lo = sbe("xt_lo", [P, KC, CW], F32R)
        work = sbe("work", [TN, 2, 2 * D])
        xc, kvn = (work[:, j, :] for j in range(2))
        lnst = sbe("lnst", [TN, 4, GR])
        hm_hi = sbe("hm_hi", [P, KC, CW], F32R)
        hm_lo = sbe("hm_lo", [P, KC, CW], F32R)
        st6 = sbe("st6", [TN, BLK, 6])
        mvs = sbe("mvs", [TN, BLK, 2])
        ve = sbe("ve", [TN, BLK])
        nm = sbe("nm", [TN, BLK])
        half = sbe("half", [TN, BLK])
        wstage = sbe("wstage", [P, KC, 2 * D])
        tab_in = sbe("tab_in", [1, 3])
        wmean = sbe("wmean", [P, KC * GR])
        w2_sb = wstage[:, :, 0:D]
        hm = wstage[:, :, D:D + CW]
        edge_phase.close()
        node_phase = ExitStack()
        sbn = alloc(node_phase)
        y_st = sbn("y_st", [P, 2, KC, CN])
        st6n = sbn("st6n", [TN, 2, 6])
        mvn = sbn("mvn", [TN, 2, 2])
        ven = sbn("ven", [TN, 2, 2])
        nmn = sbn("nmn", [TN, 2, 2])
        rst = sbn("rst", [TN, 2, 2])
        halfn = sbn("halfn", [TN, 2])
        zcol = sbn("zcol", [P, 1])
        nsum = sbn("nsum", [TN, 1])
        mrow = sbn("mrow", [1, D])
        deg_t = sbn("deg_t", [NT, TN])
        degs = sbn("degs", [TN, 3, NT])
        wr_sb = sbn("wr_sb", [P, KC, EX])
        mean_c = sbn("mean_c", [P, KC])
        rt = sbn("rt", [1, 16, EX])
        rs = sbn("rs", [1, 16])
        top_i = sbn("top_i", [1, EX], U32)
        gap = sbn("gap", [P, GAP])
        x2 = sbn("x2", [TN, NT, D])
        node_phase.close()
        sums.close()
        sbx = alloc(ctx)
        fw1_st = sbx("fw1_st", [P, 2, KC, F])
        fw2_st = sbx("fw2_st", [P, 2, FC // 2, D])
        fw1_hi = sbx("fw1_hi", [P, KC, 2 * F], F32R)
        fw1_lo = sbx("fw1_lo", [P, KC, 2 * F], F32R)
        fw2_hi = sbx("fw2_hi", [P, FC, D], F32R)
        fw2_lo = sbx("fw2_lo", [P, FC, D], F32R)
        fb1c = sbx("fb1c", [P, FC])
        fb2r = sbx("fb2r", [1, 2, D])
        grow = sbx("grow", [TN, D])
        berow = sbx("berow", [TN, D])
        b2w = sbx("b2w", [TN, D])
        wts = sbx("wts", [P, 2])
        xl = sbx("xl", [TN, 2, 2, D])
        xf_hi = sbx("xf_hi", [P, KC, CW], F32R)
        xf_lo = sbx("xf_lo", [P, KC, CW], F32R)
        h32 = sbx("h32", [P, FC, CW])
        h_hi = sbx("h_hi", [P, 2, FC, CW], F32R)
        h_lo = sbx("h_lo", [P, 2, FC, CW], F32R)
        xlb = sbx("xlb", [TN, 2, 2, D])
        xb = sbx("xb", [TN, 2, 2, D])
        o_sb = sbx("o_sb", [TN, 2, 2, D])
        res = sbx("res", [TN, 2, 2, D])
        st6x = sbx("st6x", [TN, 2, 6])
        mvx = sbx("mvx", [TN, 2, 2])
        vex = sbx("vex", [TN, 2, 2])
        nmx = sbx("nmx", [TN, 2, 2])
        rx = sbx("rx", [TN, 2, 2])
        bnx = sbx("bnx", [TN, 2, 2])
        halfx = sbx("halfx", [TN, 2])

        bank = [ctx.enter_context(nc.psum_tensor(f"bank{b}", [P, 512], F32)) for b in range(8)]
        ps_seg = [bank[0], bank[1]]
        ps_t, ps_y, ps_deg, ps_xt, ps_kv, ps_acc = bank[2:8]

        x_all = acc_y[0:TN, :, :].rearrange("p c n -> p (c n)").rearrange("p (t d) -> p t d", d=D)
        zero_blk = acc_y[:, :, :].rearrange("p c n -> p (c n)").rearrange("p (b n) -> p b n", b=NT // BLK)
        dst_i = e32[:, :, :].rearrange("p k d -> p (k d)")[:, 0:NG * GT].bitcast(I32)
        rel_tmp = e32[:, :, :].rearrange("p k d -> p (k d)")[:, NG * GT:2 * NG * GT]
        rel_g = rel[:, :].rearrange("p (g k) -> p g k", k=GT)
        slots = [range(0, HT), range(HT, GT)]

        def wide(ap, n, m):
            return ap.unsqueeze(2).broadcast_to([ap.shape[0], n, m])

        s_dst, s_src, s_wkv, s_par, s_w2 = (sem(f"s_{n}") for n in ("dst", "src", "wkv", "par", "w2"))
        s_x = [sem(f"s_x{b}") for b in range(NT // BLK)]
        s_st, s_mv, s_ps, s_r1, s_xn, s_hi16, s_lo16, s_zero = (sem(f"s_{n}") for n in (
            "st", "mv", "ps", "r1", "xn", "hi16", "lo16", "zero"))
        s_tab = [sem(f"s_tab{b}") for b in range(2)]
        s_id, s_const, s_iota, s_mask, s_d, s_dp, s_rel, s_wprep, s_wsplit = (sem(f"s_{n}") for n in (
            "id", "const", "iota", "mask", "d", "dp", "rel", "wprep", "wsplit"))
        s_e = [[sem(f"s_e{u}{h}") for h in range(2)] for u in range(2)]
        s_gat = [[sem(f"s_gat{u}{h}") for h in range(2)] for u in range(2)]
        s_idx, s_carry, s_fl, s_tp, s_flt, s_pj, s_acc, s_dacc = (sem(f"s_{n}") for n in (
            "idx", "carry", "fl", "tp", "flt", "pj", "acc", "dacc"))
        s_hot, s_ehi, s_hot16, s_elo, s_edge, s_seg = ([sem(f"s_{n}{h}") for h in range(2)] for n in (
            "hot", "ehi", "hot16", "elo", "edge", "seg"))
        s_xl = [sem(f"s_xl{u}") for u in range(2)]
        s_xst, s_xt, s_xhi, s_xlo, s_kvp, s_xc, s_sq, s_ve, s_sd, s_kd, s_kvn, s_kva = (
            sem(f"s_{n}") for n in ("xst", "xt", "xhi", "xlo", "kvp", "xc", "sq", "ve", "sd", "kd", "kvn",
                                    "kva"))
        s_c, s_ca, s_cp = (sem(f"s_{n}") for n in ("c", "ca", "cp"))
        s_mxl, s_bd = ([sem(f"s_{n}{u}") for u in range(2)] for n in ("mxl", "bd"))
        s_mst, s_hp, s_hg, s_hhi, s_hlo, s_mp, s_b1, s_bs = (
            sem(f"s_{n}") for n in ("mst", "hp", "hg", "hhi", "hlo", "mp", "b1", "bs"))
        s_pass, s_sums, s_pz, s_br, s_carry_v = (sem(f"s_{n}") for n in ("pass", "sums", "pz", "br", "carry_v"))
        s_dg, s_bl, s_rw, s_hc, s_np, s_na, s_nd, s_y, s_fs, s_fv, s_rst, s_r2, s_mean = (
            sem(f"s_{n}") for n in ("dg", "bl", "rw", "hc", "np", "na", "nd", "y", "fs", "fv", "rst", "r2", "mean"))
        s_ft, s_fx = ([sem(f"s_{n}{u}") for u in range(2)] for n in ("ft", "fx"))
        s_rd, s_rp, s_ra, s_rm, s_top = (sem(f"s_{n}") for n in ("rd", "rp", "ra", "rm", "top"))
        s_fw1, s_fw2 = ([sem(f"s_{n}{j}") for j in range(2)] for n in ("fw1", "fw2"))
        s_fb, s_wts, s_b2w, s_w1h, s_w1l, s_w2s, s_w2h, s_w2l, s_bp = (sem(f"s_{n}") for n in (
            "fb", "wts", "b2w", "w1h", "w1l", "w2s", "w2h", "w2l", "bp"))
        s_xl2, s_xtp, s_xlb, s_xb, s_g2, s_od, s_rn, s_rg, s_res, s_out = ([sem(f"s_{n}{u}") for u in range(2)] for n in (
            "xl2", "xtp", "xlb", "xb", "g2", "od", "rn", "rg", "res", "out"))
        s_xfh, s_xfl, s_g1, s_ge, s_hh, s_hl, s_xs, s_vx, s_rx, s_bnx = (sem(f"s_{n}") for n in (
            "xfh", "xfl", "g1", "ge", "hh", "hl", "xs", "vx", "rx", "bnx"))

        block = ctx.enter_context(nc.Block())
        PAIRS_KV, PAIRS_MIX, PAIRS_REST = NT // 2, NC // 2, (NG - NT - 2 * (NC // 2) - 2) // 2
        G_MIX = NT
        G_ODD = G_MIX + 2 * PAIRS_MIX
        G_REST = G_ODD + 2

        def schedule(eng, body, between, last=None):
            with eng.Fori(0, PAIRS_KV) as i:
                for u in range(2):
                    body(i * 2 + u, u, i, kv=i * 2 + u)
            between()
            with eng.Fori(0, PAIRS_MIX) as i:
                for u in range(2):
                    body(i * 2 + (G_MIX + u), u, i + G_MIX // 2, mix=i * 2 + u)
            body(G_ODD, 0, G_ODD // 2, mix=NC - 1)
            body(G_ODD + 1, 1, G_ODD // 2, put=NC - 1)
            with eng.Fori(0, PAIRS_REST - 1) as i:
                for u in range(2):
                    body(i * 2 + (G_REST + u), u, i + G_REST // 2)
            for u in range(2):
                (last or body)(NG - 2 + u, u, NG // 2 - 1, ahead=u == 0)

        def general(eng, body, start=None, epilogue=None, last=None):
            eng.wait_ge(s_rel, 1)
            ok = eng.value_load(ok_i[0:1, 0:1], min_val=0, max_val=1)
            with eng.If(ok < 1):
                with eng.Fori(1, PASSES) as k:
                    if start is not None:
                        start(k)
                    with eng.Fori(0, NG // 2 - 1) as i:
                        for u in range(2):
                            body(k * NG + (i * 2 + u), u, k * (NG // 2) + i, g=i * 2 + u)
                    for u in range(2):
                        (last or body)(k * NG + (NG - 2 + u), u, k * (NG // 2) + (NG // 2 - 1), g=NG - 2 + u, ahead=u == 0)
                if epilogue is not None:
                    epilogue(NG * PASSES)
            if epilogue is not None:
                with eng.Else():
                    epilogue(NG)

        def chunks(eng, step):
            for c in range(2):
                step(c, c, 0)
            with eng.Fori(1, NC // 2 - 1) as i:
                for u in range(2):
                    step(i * 2 + u, u, i)
            for c in range(NC - 3, NC):
                step(c, c % 2, c // 2)

        @block.sync
        def _(sp):
            sp.dma_start(e32[:, :, :].rearrange("p k d -> p (k d)")[:, 0:NG * GT].bitcast(I32), dst_l).then_inc(s_dst, 16)
            for b in range(NT // BLK):
                rows = x[b * BLK * TN:(b + 1) * BLK * TN, :].rearrange("(t p) d -> p t d", p=TN)
                for a, z in ((0, 112), (112, TN)):
                    sp.dma_start(x_all[a:z, b * BLK:(b + 1) * BLK, :], rows[a:z]).then_inc(s_x[b], 16)
                if b == 0:
                    sp.dma_start(src_sb[:, :], src_l).then_inc(s_src, 16)
                    for c in range(KC):
                        for j in range(2):
                            sp.dma_start(wstage[:, c, j * D:(j + 1) * D].rearrange("p (h e) -> p h e", e=HC),
                                         w_qkv[c * P:(c + 1) * P, :].rearrange("p (h s e) -> p h s e", s=3, e=HC)[:, :, j + 1, :]
                                         ).then_inc(s_wkv, 16)
                    for j in range(2):
                        sp.dma_start(bkv[:, j * D:(j + 1) * D].rearrange("p (h e) -> p h e", e=HC),
                                     b_qkv.rearrange("(h s e) -> h s e", s=3, e=HC)[:, j + 1, :].partition_broadcast(TN)
                                     ).then_inc(s_wkv, 16)
                    for j, row in enumerate((kln_g, vln_g, kln_b, vln_b)):
                        sp.dma_start(lns[:, j, :], row.partition_broadcast(TN)).then_inc(s_par, 16)
                    sp.dma_start(wg[:, :, :], wgnn.rearrange("(c p) d -> p c d", p=P)).then_inc(s_par, 16)
                    sp.dma_start(wq_sb[:, :, :], wq_t.rearrange("(c p) d -> p c d", p=P)).then_inc(s_par, 16)
                    sp.dma_start(bq[:, :], bq_l).then_inc(s_par, 16)
                    sp.dma_start(w1_sb[:, :, :], w1.rearrange("(c p) d -> p c d", p=P)).then_inc(s_par, 16)
                    sp.dma_start(b1c[:, :], b1_l).then_inc(s_par, 16)
                    sp.dma_start(brows[:, :], b2.partition_broadcast(TN)).then_inc(s_par, 16)
                    sp.dma_start(hrows[:, :], hbias.partition_broadcast(TN)).then_inc(s_par, 16)
            for b in range(NT // BLK):
                sp.wait_ge(s_lo16, b + 1)
                rows = table[b * BLK * TN:(b + 1) * BLK * TN, :].rearrange("(t p) d -> p t d", p=TN)
                o = (b % 2) * BLK
                for a, z in ((0, 112), (112, TN)):
                    sp.dma_start(rows[a:z], gring[a:z, o:o + BLK, :]).then_inc(s_tab[b % 2], 16)
            sp.wait_ge(s_wsplit, 2)
            sp.dma_start(w2_sb, w2.rearrange("(c p) d -> p c d", p=P)).then_inc(s_w2, 16)
            sp.wait_ge(s_rel, 1)

            def load_group(it, u, pair, start, kv, mix):
                rows = edges[ds(start, GE), :].rearrange("(p k) d -> p k d", k=GT)
                if kv is not None:
                    xr = x[ds(kv * TN, TN), :]
                if mix is not None:
                    xr = x[ds(mix * CN, CN), :].rearrange("(t p) d -> p t d", p=TN)
                for h in range(2):
                    part = rows[:, h * HT:(h + 1) * HT, :]
                    sp.wait_ge(s_elo[h], fin(it, 1))
                    sp.dma_start(e32[:, h * HT:(h + 1) * HT, :], part).then_inc(s_e[u][h], 16)
                if kv is not None:
                    sp.wait_ge(s_xst, fin(kv, 2))
                    sp.dma_start(xch[:, u, 0, :], xr).then_inc(s_xl[u], 16)
                if mix is not None:
                    sp.wait_ge(s_bd[u], (pair + (1 - G_MIX // 2)) * 16)
                    sp.dma_start(xch[:, u, :, :], xr).then_inc(s_mxl[u], 16)

            def body(it, u, pair, kv=None, mix=None, g=None, ahead=True, put=None):
                load_group(it, u, pair, (it if g is None else g) * GE, kv, mix)

            def last(it, u, pair, g=None, ahead=True):
                load_group(it, u, pair, (NG - 2) * GE if u == 0 else LAST, None, None)

            def between():
                sp.wait_ge(s_xst, NT + 2)

            schedule(sp, body, between, last)
            general(sp, body, last=last)

            sp.wait_ge(s_sums, 1)
            sp.dma_start(deg_d, deg_row[0:1, 0:N]).then_inc(s_dg, 16)
            sp.wait_ge(s_dg, 16)
            sp.dma_start(deg_t[:, :], deg_d.rearrange("o (t p) -> (o t) p", p=TN)).then_inc(s_dg, 16)
            sp.wait_ge(s_bd[0], 16 * (NC - NC // 2 + 1))
            sp.wait_ge(s_bd[1], 16 * (NC // 2 + 1))
            for b in range(NT // BLK):
                rows = base_d[CN + b * BLK * TN:CN + (b + 1) * BLK * TN, :].rearrange("(t p) d -> p t d", p=TN)
                for a, z in ((0, 112), (112, TN)):
                    sp.dma_start(x2[a:z, b * BLK:(b + 1) * BLK, :], rows[a:z]).then_inc(s_bl, 16)
            sp.dma_start(wr_sb[:, :, :], wr.rearrange("(c p) e -> p c e", p=P)).then_inc(s_rw, 16)
            sp.dma_start(rt[0:1, 0, :], br.partition_broadcast(1)).then_inc(s_rw, 16)
            sp.wait_ge(s_top, 1)
            chosen = [sp.value_load(top_i[0:1, j:j + 1], min_val=0, max_val=EX - 1) for j in range(2)]
            for j, e in enumerate(chosen):
                sp.dma_start(fw1_st[:, j, :, :], fw1[ds(e, 1), :, :].rearrange("e (c p) f -> p (e c) f", p=P)).then_inc(s_fw1[j], 16)
            for j, e in enumerate(chosen):
                sp.dma_start(fb1c[:, j * (FC // 2):(j + 1) * (FC // 2)],
                             fb1_l[ds(e, 1), :, :].rearrange("e p f -> p (e f)")).then_inc(s_fb, 16)
                sp.dma_start(fb2r[0:1, j, :], fb2[ds(e, 1), :]).then_inc(s_fb, 16)
            for j, e in enumerate(chosen):
                sp.dma_start(fw2_st[:, j, :, :], fw2[ds(e, 1), :, :].rearrange("e (f p) d -> p (e f) d", p=P)).then_inc(s_fw2[j], 16)
            sp.dma_start(grow[:, :], gamma.partition_broadcast(TN)).then_inc(s_fb, 16)
            sp.dma_start(berow[:, :], beta.partition_broadcast(TN)).then_inc(s_fb, 16)

            def store(c, u, i):
                rows = out[ds(c * CN, CN), :].rearrange("(t p) d -> p t d", p=TN)
                sp.wait_ge(s_res[u], i + 1)
                sp.dma_start(rows, res[:, u, :, :]).then_inc(s_out[u], 16)

            with sp.Fori(0, NC // 2) as i:
                for u in range(2):
                    store(i * 2 + u, u, i)
            store(NC - 1, 0, NC // 2)
            sp.wait_ge(s_out[0], 16 * (NC - NC // 2))
            sp.wait_ge(s_out[1], 16 * (NC // 2))

        @block.gpsimd
        def _(pool):
            pool.memset(ident[:, :], 0.0).then_inc(s_id, 1)
            pool.memset(ones[:, :], 1.0).then_inc(s_const, 1)
            pool.wait_ge(s_id, 1)
            pool.affine_select(out=ident[:, :], in_=ident[:, :], compare_op=ALU.not_equal, fill=1.0, base=0,
                               pattern=[[-1, P]], channel_multiplier=1).then_inc(s_id, 1)
            pool.memset(ones16[:, :], 1.0).then_inc(s_const, 1)
            pool.memset(half[:, :], -0.5).then_inc(s_const, 1)
            pool.memset(xch[:, 1, 1, :], 0.0).then_inc(s_const, 1)
            pool.memset(tab_in[:, :], 1.0).then_inc(s_const, 1)
            pool.iota(iota_i[:, :], [[1, W]], base=0, channel_multiplier=0).then_inc(s_iota, 1)
            pool.memset(block_mask[:, :], 0.0).then_inc(s_mask, 1)
            pool.wait_ge(s_mask, 1)
            for j in range(P // HC):
                pool.memset(block_mask[j * HC:(j + 1) * HC, j * HC:(j + 1) * HC], 1.0 / N).then_inc(s_mask, 1)
            pool.wait_ge(s_mask, 1 + P // HC)
            pool.memset(kvn, 0.0).then_inc(s_const, 1)
            for t in (xt_hi, xt_lo, hm_hi, hm_lo):
                pool.memset(t[:, :, :].bitcast(F32), 0.0).then_inc(s_const, 1)
            pool.memset(deg_row[:, :], 0.0).then_inc(s_zero, 1)

            def small(b):
                pool.wait_ge(s_mv, BLK * (b + 1))
                pool.tensor_scalar(ve[:, :], mvs[:, :, 1], EPS, None, ALU.add).then_inc(s_ps, 1)
                if b:
                    pool.wait_ge(s_r1, b)
                pool.tensor_scalar(nm[:, :], mvs[:, :, 0], -1.0, None, ALU.mult).then_inc(s_ps, 1)
                pool.wait_ge(s_ps, 3 * b + 2)
                pool.tensor_tensor(r1[:, ds(b * BLK, BLK)], ve[:, :], half[:, :], ALU.pow).then_inc(s_ps, 1)
                pool.wait_ge(s_ps, 3 * b + 3)
                pool.tensor_tensor(nmr1[:, ds(b * BLK, BLK)], nm[:, :], r1[:, ds(b * BLK, BLK)],
                                   ALU.mult).then_inc(s_r1, 1)

            def zero(b):
                pool.wait_ge(s_lo16, b + 1)
                pool.memset(zero_blk[:, ds(b, 1), :] if not isinstance(b, int) else zero_blk[:, b:b + 1, :],
                            0.0).then_inc(s_zero, 1)

            pool.wait_ge(s_const, 10)
            for b in range(NT // BLK):
                small(b)
                if b:
                    zero(b - 1)
            zero(NT // BLK - 1)
            for b in range(NT // BLK):
                pool.wait_ge(s_tab[b % 2], 32 * (b // 2 + 1))

            def body(it, u, pair, kv=None, mix=None, g=None, ahead=True, put=None):
                g = it if g is None else g
                for h in range(2):
                    a = u * GT + h * HT
                    pool.wait_ge(s_seg[h], fin(it, 2))
                    pool.sem_inc(s_carry, 1)
                    pool.tensor_copy(idx[:, a:a + HT], src_sb[:, ds(g * GT + h * HT, HT)]).then_inc(s_idx, 1)
                    pool.wait_ge(s_idx, it * 2 + (h + 1))
                    pool.sem_inc(s_carry, 1)
                    for k in range(a, a + HT):
                        pool.indirect_dma_start(
                            out=gring[:, k, :], out_offset=None, in_=table,
                            in_offset=bass.IndirectOffsetOnAxis(ap=idx[:, k:k + 1], axis=0),
                        ).then_inc(s_gat[u][h], 16)

            pool.wait_ge(s_src, 16)
            with pool.Fori(0, NG // 2) as i:
                for u in range(2):
                    body(i * 2 + u, u, i)
            general(pool, body)

            pool.sem_inc(s_r2, 4)
            pool.wait_ge(s_sums, 1)
            pool.memset(halfn[:, :], -0.5).then_inc(s_hc, 1)
            pool.wait_ge(s_hc, 1)

            def scales(c, u, i):
                pool.wait_ge(s_fv, c * 2 + 2)
                pool.wait_ge(s_r2, c * 2 + 4)
                pool.tensor_tensor(rst[:, u, :], ven[:, u, :], halfn[:, :], ALU.pow).then_inc(s_rst, 1)
                pool.wait_ge(s_rst, c + 1)
                pool.tensor_copy(r2[:, ds(c * 2, 2)], rst[:, u, :]).then_inc(s_r2, 1)
                pool.tensor_tensor(nmr2[:, ds(c * 2, 2)], nmn[:, u, :], rst[:, u, :], ALU.mult).then_inc(s_r2, 1)

            scales(0, 0, 0)
            with pool.Fori(0, NC // 2) as i:
                for u in range(2):
                    scales(i * 2 + (1 + u), 1 - u, i)

            pool.wait_ge(s_top, 1)
            pool.memset(halfx[:, :], -0.5).then_inc(s_hc, 1)
            pool.wait_ge(s_hc, 2)
            pool.wait_ge(s_b2w, 1)
            pool.wait_ge(s_fb, 16 * 6)

            def residual(c, u, i):
                pool.wait_ge(s_xl2[u], i * 2 + 2)
                wait_past(pool, s_od[u], i)
                pool.tensor_tensor(xlb[:, u, :, :], xl[:, u, :, :], b2w[:, :].unsqueeze(1).broadcast_to([TN, 2, D]),
                                   ALU.add).then_inc(s_xlb[u], 1)

            def step(c, u, i):
                if not (isinstance(c, int) and c + 1 >= NC):
                    residual(c + 1, 1 - u, i + u)
                wait_past(pool, s_res[u], i)
                pool.tensor_tensor(xb[:, u, :, :], x2[:, ds(c * 2, 2), :], berow[:, :].unsqueeze(1).broadcast_to([TN, 2, D]),
                                   ALU.add).then_inc(s_xb[u], 1)
                pool.wait_ge(s_vx, c * 2 + 2)
                wait_past(pool, s_bnx, c)
                pool.tensor_tensor(rx[:, u, :], vex[:, u, :], halfx[:, :], ALU.pow).then_inc(s_rx, 1)
                pool.wait_ge(s_rx, c + 1)
                pool.tensor_tensor(bnx[:, u, :], nmx[:, u, :], rx[:, u, :], ALU.mult).then_inc(s_bnx, 1)

            residual(0, 0, 0)
            chunks(pool, step)

        @block.scalar
        def _(act):
            def copy(o, i):
                return nc.scalar.activation(o, i, ACT.Copy)

            act.sem_inc(s_ehi[0], 2)
            act.sem_inc(s_ehi[1], 2)
            act.sem_inc(s_hot16[0], 2)
            act.sem_inc(s_hot16[1], 2)
            act.sem_inc(s_fl, 1)
            act.sem_inc(s_flt, 1)
            act.sem_inc(s_bd[0], 16)
            for s in (s_xst, s_xhi, s_sq, s_sd, s_hg, s_hhi):
                act.sem_inc(s, 2)
            for b in range(NT // BLK):
                act.wait_ge(s_r1, b + 1)
                for j in range(BLK):
                    t = b * BLK + j
                    nc.scalar.activation(x_all[:, t, :], x_all[:, t, :], ACT.Identity, bias=nmr1[:, t:t + 1],
                                         scale=r1[:, t:t + 1]).then_inc(s_xn, 1)
                act.wait_ge(s_xn, BLK * (b + 1))
                if b >= 2:
                    act.wait_ge(s_tab[b % 2], 32 * (b // 2))
                o = (b % 2) * BLK
                copy(gring[0:TN, o:o + BLK, 0:D], x_all[:, b * BLK:(b + 1) * BLK, :]).then_inc(s_hi16, 1)
            act.wait_ge(s_wprep, 2)
            copy(wkv_hi[:, :, :], wstage[:, :, :]).then_inc(s_wsplit, 1)
            act.wait_ge(s_w2, 16)
            copy(w2_hi[:, :, :], w2_sb).then_inc(s_ca, 1)
            act.wait_ge(s_const, 10)
            nc.scalar.activation(tab_in[:, 1:2], tab_in[:, 0:1], ACT.Sqrt)
            act.wait_ge(s_pz, 2)

            def flush(it, u):
                act.wait_ge(s_seg[1], fin(it, 1))
                act.wait_ge(s_tp, fin(it, 2))
                copy(fl[:, :], ps_seg[1 - u][:, :]).then_inc(s_fl, 1)

            def flush_t(it):
                act.wait_ge(s_tp, fin(it, 1))
                act.wait_ge(s_pj, fin(it, 2))
                copy(fl_t[:, :, :], ps_t[:, :].rearrange("p (c n) -> p c n", c=4)).then_inc(s_flt, 1)

            def epilogue(it):
                flush(it, 0)
                flush_t(it)

            def prepare(it, u, pair, h):
                act.wait_ge(s_e[u][h], 16 * (pair + 1))
                act.wait_ge(s_edge[h], fin(it, 1))
                copy(e_hi[:, h * HT:(h + 1) * HT, :], e32[:, h * HT:(h + 1) * HT, :]).then_inc(s_ehi[h], 1)

            def prepare16(it, h):
                act.wait_ge(s_hot[h], fin(it))
                act.wait_ge(s_seg[h], fin(it, 1))
                act.wait_ge(s_edge[1], fin(it, 1))
                copy(s16[:, h * HT:(h + 1) * HT, :], s32[:, h * HT:(h + 1) * HT, :].bitcast(F32)).then_inc(s_hot16[h], 1)

            def first_half(it, pair):
                prepare(it, 0, pair, 0)
                prepare16(it, 0)

            def body(it, u, pair, kv=None, mix=None, g=None, ahead=True, put=None):
                if kv is not None:
                    act.wait_ge(s_xl[u], 16 * (pair + 1))
                    act.wait_ge(s_xt, fin(kv, 1))
                    nc.scalar.activation(xnc[:, 0, :], xch[:, u, 0, :], ACT.Identity, bias=nmr1[:, ds(kv, 1)],
                                         scale=r1[:, ds(kv, 1)]).then_inc(s_xst, 1)
                if mix is not None:
                    act.wait_ge(s_mxl[u], 16 * (pair + (1 - G_MIX // 2)))
                    act.wait_ge(s_bs, fin(mix, 1))
                    for j in range(2):
                        nc.scalar.activation(xnc[:, j, :], xch[:, u, j, :], ACT.Identity, bias=nmr1[:, ds(mix * 2 + j, 1)],
                                             scale=r1[:, ds(mix * 2 + j, 1)]).then_inc(s_mst, 1)
                    put = mix - 1
                if put is not None:
                    if mix is None:
                        act.wait_ge(s_bs, fin(put))
                    act.dma_start(base_d[ds(put * CN + CN, CN), :].rearrange("(t p) d -> p t d", p=TN),
                                  xch[:, 1 - u, :, :]).then_inc(s_bd[1 - u], 16)
                flush(it, u)
                prepare(it, u, pair, 1)
                prepare16(it, 1)
                if kv is not None:
                    act.wait_ge(s_xt, fin(kv))
                    act.wait_ge(s_kvp, fin(kv, 1))
                    copy(xt_hi[:, :, 0:TN], ps_xt[:, 0:KC * TN].rearrange("p (c n) -> p c n", c=KC)).then_inc(s_xhi, 1)
                if mix is not None:
                    act.wait_ge(s_xt, fin(mix + NT))
                    act.wait_ge(s_hp, fin(mix, 1))
                    copy(xt_hi[:, :, 0:CN], ps_xt[:, 0:KC * CN].rearrange("p (c n) -> p c n", c=KC)).then_inc(s_xhi, 1)
                flush_t(it)
                if mix is not None:
                    act.wait_ge(s_hp, fin(mix))
                    act.wait_ge(s_hlo, fin(mix, 1))
                    for f in range(KC):
                        gelu = nc.scalar.activation(hm[:, f, 0:CN], ps_kv[:, f * CW:f * CW + CN], ACT.Gelu, bias=bm[:, f:f + 1])
                    gelu.then_inc(s_hg, 1)
                    act.wait_ge(s_hg, fin(mix))
                    act.wait_ge(s_mp, fin(mix, 1))
                    copy(hm_hi[:, :, 0:CN], hm[:, :, 0:CN]).then_inc(s_hhi, 1)
                if ahead:
                    prepare(it + 1, 1 - u, pair + u, 0)
                if kv is not None:
                    act.wait_ge(s_xc, fin(kv))
                    act.wait_ge(s_kva, fin(kv))
                    nc.scalar.activation(kvn, xc, ACT.Square).then_inc(s_sq, 1)
                    act.wait_ge(s_ve, fin(kv))
                    nc.scalar.activation(lnst[:, 2, :], lnst[:, 1, :], ACT.Sqrt).then_inc(s_sd, 1)
                if ahead:
                    prepare16(it + 1, 0)

            def between():
                nc.scalar.activation(tab_in[:, 2:3], tab_in[:, 0:1], ACT.Gelu)
                act.wait_ge(s_c, 3)
                copy(m_hi[:, :, :], p_sb[:, :, :]).then_inc(s_ca, 1)

            first_half(0, 0)
            schedule(act, body, between)
            general(act, body, lambda k: first_half(k * NG, k * (NG // 2)), epilogue)

            act.wait_ge(s_sums, 1)
            act.wait_ge(s_nd, 2)
            nc.scalar.activation(degs[:, 1, :], degs[:, 0, :], ACT.Sqrt).then_inc(s_na, 1)

            def stage(c, u, i):
                act.wait_ge(s_ft[u], i + 1)
                copy(y_st[:, u, :, :], acc_y[:, :, ds(c * CN, CN)]).then_inc(s_y, 1)

            stage(0, 0, 0)
            with act.Fori(0, NC // 2) as i:
                for u in range(2):
                    stage(i * 2 + (1 + u), 1 - u, i + u)

            act.wait_ge(s_rd, 5)
            nc.scalar.activation(rt[0:1, 2, :], rt[0:1, 1, :], ACT.Exp, bias=rs[0:1, 1:2]).then_inc(s_ra, 1)
            act.wait_ge(s_rd, 16)
            nc.scalar.activation(rt[0:1, 9, :], rt[0:1, 8, :], ACT.Exp, bias=rs[0:1, 5:6]).then_inc(s_ra, 1)
            act.wait_ge(s_rd, 21)
            nc.scalar.activation(rt[0:1, 12, 0:2], rt[0:1, 11, 0:2], ACT.Exp, bias=rs[0:1, 8:9]).then_inc(s_ra, 1)

            for j in range(2):
                act.wait_ge(s_fw1[j], 16)
                copy(fw1_hi[:, :, j * F:(j + 1) * F], fw1_st[:, j, :, :]).then_inc(s_w1h, 1)
            for j in range(2):
                act.wait_ge(s_w2s, j + 1)
                copy(fw2_hi[:, j * (FC // 2):(j + 1) * (FC // 2), :], fw2_st[:, j, :, :]).then_inc(s_w2h, 1)
            act.wait_ge(s_fb, 16 * 6)

            def rows(c, u, i):
                wait_past(act, s_xlb[u], i)
                wait_past(act, s_xtp[u], i)
                for j in range(2):
                    nc.scalar.activation(xl[:, u, j, :], x2[:, ds(c * 2 + j, 1), :], ACT.Identity, bias=nmr2[:, ds(c * 2 + j, 1)],
                                         scale=r2[:, ds(c * 2 + j, 1)]).then_inc(s_xl2[u], 1)

            def rows_hi(c, u, i):
                act.wait_ge(s_xtp[u], i + 1)
                copy(xf_hi[:, :, 0:CN], ps_xt[:, 0:KC * CN].rearrange("p (c n) -> p c n", c=KC)).then_inc(s_xfh, 1)

            def hidden(c, u, i):
                for q in range(FC // 2):
                    act.wait_ge(s_g1, c * (FC // 2) + (q + 1))
                    if not (isinstance(c, int) and c == 0):
                        act.wait_ge(s_hl, c * (FC // 2) + (q + 1 - FC // 2))
                    for f in range(2 * q, 2 * q + 2):
                        nc.scalar.activation(h32[:, f, :], bank[q][:, (f % 2) * CW:(f % 2 + 1) * CW], ACT.Gelu,
                                             bias=fb1c[:, f:f + 1]).then_inc(s_ge, 1)
                    act.wait_ge(s_ge, c * FC + (2 * q + 2))
                    wait_past(act, s_g2[u], i)
                    copy(h_hi[:, u, 2 * q:2 * q + 2, :], h32[:, 2 * q:2 * q + 2, :]).then_inc(s_hh, 1)

            def normed(c, u, i):
                act.wait_ge(s_bnx, c + 1)
                wait_past(act, s_out[u], i * 16)
                for j in range(2):
                    nc.scalar.activation(res[:, u, j, :], o_sb[:, u, j, :], ACT.Identity, bias=bnx[:, u, j:j + 1],
                                         scale=rx[:, u, j:j + 1]).then_inc(s_rn[u], 1)

            def step(c, u, i):
                fixed = isinstance(c, int)
                if not (fixed and c + 2 >= NC):
                    rows(c + 2, u, i + 1)
                if not (fixed and c + 1 >= NC):
                    hidden(c + 1, 1 - u, i + u)
                if not (fixed and c + 2 >= NC):
                    rows_hi(c + 2, u, i + 1)
                if not (fixed and c == 0):
                    normed(c - 1, 1 - u, i + (u - 1))

            rows(0, 0, 0)
            rows_hi(0, 0, 0)
            rows(1, 1, 0)
            hidden(0, 0, 0)
            rows_hi(1, 1, 0)
            chunks(act, step)
            normed(NC - 1, (NC - 1) % 2, NC // 2)

        @block.tensor
        def _(pe):
            pe.sem_inc(s_seg[0], 2)
            pe.sem_inc(s_seg[1], 2)
            pe.sem_inc(s_edge[0], 2)
            pe.sem_inc(s_edge[1], 2)
            pe.sem_inc(s_tp, 1)
            pe.sem_inc(s_pj, 1)
            for s in (s_xt, s_kvp, s_kva, s_hp, s_mp):
                pe.sem_inc(s, 2)
            pe.wait_ge(s_id, 2)
            pe.wait_ge(s_const, 10)
            pe.wait_ge(s_d, 2)
            pe.transpose(ps_t[0:NG, 0:P], gmin[:, :], ident[:, :]).then_inc(s_dp, 1)
            pe.wait_ge(s_d, 4)
            pe.matmul(ps_y[:, 0:NG], lhsT=bcol_w[:, :], rhs=ident[0:NG, 0:NG], start=True, stop=True).then_inc(s_dp, 1)
            pe.wait_ge(s_d, 8)
            pe.transpose(ps_t[0:1, 0:P], okc[:, 0:1], ident[:, :]).then_inc(s_dp, 1)
            pe.wait_ge(s_d, 10)
            pe.matmul(ps_xt[:, 0:1], lhsT=ones[0:1, :], rhs=okc[0:1, 2:3], start=True, stop=True).then_inc(s_dp, 1)
            pe.matmul(ps_acc[:, 0:KC * P], lhsT=xt_hi[:, 0, 0:P], rhs=xt_lo[:, 0, :], start=True, stop=True, skip_group_check=True)
            pe.wait_ge(s_par, 16 * 11)
            pe.wait_ge(s_wsplit, 2)
            pe.wait_ge(s_d, 12)

            def products(hi, lo):
                return ((hi[0], hi[1]), (hi[0], lo[1]), (lo[0], hi[1]))

            def transposes(it):
                pe.wait_ge(s_fl, fin(it, 1))
                pe.wait_ge(s_flt, fin(it, 2))
                for c in range(4):
                    mm = pe.transpose(ps_t[:, c * W:(c + 1) * W], fl[:, c * P:(c + 1) * P], ident[:, :])
                mm.then_inc(s_tp, 1)

            def project(it):
                pe.wait_ge(s_flt, fin(it, 1))
                pe.wait_ge(s_acc, fin(it, 2))
                for o in range(KC):
                    for c in range(4):
                        mm = pe.matmul(ps_y[:, o * W:(o + 1) * W], lhsT=wg[:, c, o * P:(o + 1) * P], rhs=fl_t[:, c, :],
                                       start=c == 0, stop=c == 3)
                mm.then_inc(s_pj, 1)

            def epilogue(it):
                transposes(it)
                project(it)

            def edge_part(it, u, h):
                pe.wait_ge(s_hot[h], fin(it))
                pe.wait_ge(s_ehi[h], fin(it))
                if h == 1:
                    pe.wait_ge(s_hot16[0], fin(it))
                    pe.wait_ge(s_hot16[1], fin(it))
                    pe.wait_ge(s_dacc, fin(it, 1))
                    for k in range(GT):
                        pe.matmul(ps_deg[0:1, 0:W], lhsT=ones16[:, :], rhs=s16[:, k, :], start=k == 0, stop=k == GT - 1)
                if h == 0:
                    pe.wait_ge(s_fl, fin(it, 2))
                for k in slots[h]:
                    pe.matmul(ps_seg[u][:, D:2 * D], lhsT=s32[:, k, :], rhs=e_hi[:, k, :], start=k == 0, stop=False, skip_group_check=True)
                pe.wait_ge(s_elo[h], fin(it))
                for k in slots[h]:
                    mm = pe.matmul(ps_seg[u][:, D:2 * D], lhsT=s32[:, k, :], rhs=e_lo[:, k, :], start=False, stop=k == GT - 1, skip_group_check=True)
                mm.then_inc(s_edge[h], 1)

            def x_part(it, u, pair, h):
                pe.wait_ge(s_hot16[h], fin(it))
                pe.wait_ge(s_gat[u][h], (pair + 1) * (16 * HT))
                for k in slots[h]:
                    for j in range(2):
                        mm = pe.matmul(ps_seg[u][:, 0:D], lhsT=s16[:, k, :], rhs=gring[:, u * GT + k, j * D:(j + 1) * D],
                                       start=False, stop=k == GT - 1 and j == 1, skip_group_check=True)
                mm.then_inc(s_seg[h], 1)

            def accumulate():
                for h in range(KC):
                    mm = pe.matmul(ps_acc[:, h * P:(h + 1) * P], lhsT=kvn[:, D + h * P:D + (h + 1) * P], rhs=kvn[:, h * P:(h + 1) * P],
                                   start=False, stop=True, skip_group_check=True)
                mm.then_inc(s_kva, 1)

            def body(it, u, pair, kv=None, mix=None, g=None, ahead=True, put=None):
                edge_part(it, u, 0)
                if kv is not None:
                    pe.wait_ge(s_kvn, fin(kv, 1))
                    accumulate()
                    pe.wait_ge(s_xst, fin(kv))
                    pe.wait_ge(s_xlo, fin(kv, 1))
                    for c in range(KC):
                        mm = pe.transpose(ps_xt[:, c * TN:(c + 1) * TN], xnc[:, 0, c * P:(c + 1) * P], ident[0:TN, 0:TN])
                    mm.then_inc(s_xt, 1)
                if mix is not None:
                    pe.wait_ge(s_mst, mix * 2 + 2)
                    pe.wait_ge(s_xlo, fin(mix + NT, 1))
                    for j in range(2):
                        for c in range(KC):
                            mm = pe.transpose(ps_xt[:, c * CN + j * TN:c * CN + (j + 1) * TN], xnc[:, j, c * P:(c + 1) * P], ident[0:TN, 0:TN])
                    mm.then_inc(s_xt, 1)
                x_part(it, u, pair, 0)
                transposes(it)
                if kv is not None:
                    pe.wait_ge(s_xhi, fin(kv))
                    pe.wait_ge(s_xlo, fin(kv))
                    pe.wait_ge(s_xc, fin(kv, 1))
                    ops = [(a[:, c, 0:TN], b[:, c, :]) for c in range(KC) for a, b in products((xt_hi, wkv_hi), (xt_lo, wkv_lo))]
                    for n, (a, b) in enumerate(ops):
                        mm = pe.matmul(ps_kv[0:TN, :], lhsT=a, rhs=b, start=n == 0, stop=n == len(ops) - 1)
                    mm.then_inc(s_kvp, 1)
                if mix is not None:
                    pe.wait_ge(s_xhi, fin(mix + NT))
                    pe.wait_ge(s_xlo, fin(mix + NT))
                    pe.wait_ge(s_hg, fin(mix, 1))
                    for f in range(KC):
                        ops = [(a[:, c, f * P:(f + 1) * P], b[:, c, :]) for c in range(KC) for a, b in products((m_hi, xt_hi), (m_lo, xt_lo))]
                        for n, (a, b) in enumerate(ops):
                            mm = pe.matmul(ps_kv[:, f * CW:(f + 1) * CW], lhsT=a, rhs=b, start=n == 0, stop=n == len(ops) - 1)
                    mm.then_inc(s_hp, 1)
                project(it)
                edge_part(it, u, 1)
                if mix is not None:
                    pe.wait_ge(s_hhi, fin(mix))
                    pe.wait_ge(s_hlo, fin(mix))
                    pe.wait_ge(s_bs, fin(mix, 1))
                    for j in range(2):
                        ops = [(a[:, f, j * TN:(j + 1) * TN], b[:, f, :]) for f in range(KC) for a, b in products((hm_hi, w2_hi), (hm_lo, w2_lo))]
                        for n, (a, b) in enumerate(ops):
                            mm = pe.matmul(ps_acc[0:TN, j * D:(j + 1) * D], lhsT=a, rhs=b, start=n == 0, stop=n == len(ops) - 1)
                    mm.then_inc(s_mp, 1)
                x_part(it, u, pair, 1)

            def between():
                pe.wait_ge(s_kvn, NT + 2)
                accumulate()
                pe.wait_ge(s_c, 1)
                for h in range(KC):
                    mm = pe.matmul(ps_kv[:, h * D:(h + 1) * D], lhsT=kv_t[:, h, :], rhs=w1_sb[:, h, :], start=True, stop=True)
                mm.then_inc(s_cp, 1)
                pe.wait_ge(s_c, 2)
                pe.wait_ge(s_xlo, NT + 2)
                for o in range(KC):
                    for c in range(KC):
                        pe.matmul(ps_xt[:, o * D:(o + 1) * D], lhsT=wq_sb[:, c, o * P:(o + 1) * P], rhs=p_sb[:, c, :], start=c == 0, stop=c == KC - 1)
                for f in range(KC):
                    for c in range(KC):
                        mm = pe.matmul(ps_acc[:, f:f + 1], lhsT=p_sb[:, c, f * P:(f + 1) * P], rhs=bq[:, c:c + 1], start=c == 0, stop=c == KC - 1)
                mm.then_inc(s_cp, 1)
                pe.wait_ge(s_c, 6)
                pe.wait_ge(s_ca, 2)

            schedule(pe, body, between)
            general(pe, body, epilogue=epilogue)

            pe.wait_ge(s_sums, 1)
            pe.wait_ge(s_dg, 32)
            pe.transpose(ps_t[0:TN, 0:NT], deg_t[:, :], ident[0:NT, 0:NT]).then_inc(s_np, 1)
            pe.sem_inc(s_ft[0], 1)
            pe.sem_inc(s_ft[1], 1)
            ps_mean = ps_kv
            pe.wait_ge(s_nd, 1)
            for c in range(KC):
                pe.matmul(ps_mean[0:1, c * P:(c + 1) * P], lhsT=zcol[:, :], rhs=ones[:, :], start=c == 0, stop=True, skip_group_check=True)

            def rows(c, u, i):
                pe.wait_ge(s_y, c + 1)
                pe.wait_ge(s_fx[u], i * 2 + 2)
                for j in range(2):
                    for o in range(KC):
                        mm = pe.transpose(bank[u][0:TN, j * D + o * P:j * D + (o + 1) * P], y_st[:, u, o, j * TN:(j + 1) * TN], ident[:, :])
                mm.then_inc(s_ft[u], 1)

            def mean(c, u):
                pe.wait_ge(s_rst, c + 1)
                for j in range(2):
                    mm = pe.matmul(ps_mean[0:1, 0:D], lhsT=rst[:, u, j:j + 1], rhs=x2[:, ds(c * 2 + j, 1), :], start=False, stop=True, skip_group_check=True)
                mm.then_inc(s_mean, 1)

            rows(0, 0, 0)
            with pe.Fori(0, NC // 2) as i:
                for u in range(2):
                    rows(i * 2 + (1 + u), 1 - u, i + u)
                    mean(i * 2 + u, u)
            mean(NC - 1, 0)
            pe.wait_ge(s_rd, 1)
            pe.matmul(ps_t[0:1, 0:1], lhsT=nsum[:, :], rhs=ones[0:TN, 0:1], start=True, stop=True).then_inc(s_rp, 1)
            pe.wait_ge(s_rd, 2 + 1)
            for c in range(KC):
                mm = pe.matmul(ps_xt[:, c:c + 1], lhsT=mrow[0:1, c * P:(c + 1) * P], rhs=ones[0:1, 0:1], start=True, stop=True)
            mm.then_inc(s_rp, 1)
            pe.wait_ge(s_rm, 1)
            pe.wait_ge(s_rw, 32)
            for c in range(KC):
                mm = pe.matmul(ps_t[0:1, 0:EX], lhsT=mean_c[:, c:c + 1], rhs=wr_sb[:, c, :], start=c == 0, stop=c == KC - 1)
            mm.then_inc(s_rp, 1)
            pe.wait_ge(s_top, 2)
            pe.matmul(ps_y[:, 0:2], lhsT=ones[0:1, :], rhs=rt[0:1, 13, 0:2], start=True, stop=True).then_inc(s_bp, 1)
            pe.wait_ge(s_w2s, 4)
            for j in range(2):
                mm = pe.matmul(ps_acc[0:TN, 0:D], lhsT=ones[0:1, 0:TN], rhs=fb2r[0:1, j, :], start=j == 0, stop=j == 1)
            mm.then_inc(s_bp, 1)

            ps_o = [ps_kv, ps_acc]

            def turn(c, u, i):
                pe.wait_ge(s_xl2[u], i * 2 + 2)
                wait_past(pe, s_xfl, c)
                for j in range(2):
                    for o in range(KC):
                        mm = pe.transpose(ps_xt[:, o * CN + j * TN:o * CN + (j + 1) * TN], xl[:, u, j, o * P:(o + 1) * P], ident[0:TN, 0:TN])
                mm.then_inc(s_xtp[u], 1)

            def first(c, u, i):
                pe.wait_ge(s_xfh, c + 1)
                pe.wait_ge(s_xfl, c + 1)
                for f in range(FC):
                    q = f // 2
                    if f % 2 == 0 and not (isinstance(c, int) and c == 0):
                        pe.wait_ge(s_ge, c * FC + (2 * q + 2 - FC))
                    ops = [(a[:, k, f * P:(f + 1) * P], b[:, k, :]) for k in range(KC) for a, b in products((fw1_hi, xf_hi), (fw1_lo, xf_lo))]
                    for n, (a, b) in enumerate(ops):
                        mm = pe.matmul(bank[q][:, (f % 2) * CW:(f % 2 + 1) * CW], lhsT=a, rhs=b, start=n == 0, stop=n == len(ops) - 1)
                    if f % 2:
                        mm.then_inc(s_g1, 1)

            def second(c, u, i):
                pe.wait_ge(s_hh, c * (FC // 2) + FC // 2)
                pe.wait_ge(s_hl, c * (FC // 2) + FC // 2)
                wait_past(pe, s_od[u], i)
                for j in range(2):
                    ops = [(a[:, u, f, j * TN:(j + 1) * TN], b[:, f, :]) for f in range(FC) for a, b in products((h_hi, fw2_hi), (h_lo, fw2_lo))]
                    for n, (a, b) in enumerate(ops):
                        mm = pe.matmul(ps_o[u][0:TN, j * D:(j + 1) * D], lhsT=a, rhs=b, start=n == 0, stop=n == len(ops) - 1)
                mm.then_inc(s_g2[u], 1)

            def step(c, u, i):
                fixed = isinstance(c, int)
                if not (fixed and c + 1 >= NC):
                    first(c + 1, 1 - u, i + u)
                if not (fixed and c + 2 >= NC):
                    turn(c + 2, u, i + 1)
                second(c, u, i)

            turn(0, 0, 0)
            pe.wait_ge(s_w1l, 4)
            first(0, 0, 0)
            turn(1, 1, 0)
            pe.wait_ge(s_w2l, 2)
            pe.wait_ge(s_b2w, 1)
            chunks(pe, step)

        @block.vector
        def _(v):
            for s in (s_hot[0], s_hot[1], s_elo[0], s_elo[1], s_xlo, s_xc, s_ve, s_kvn, s_hlo, s_bs):
                v.sem_inc(s, 2)
            v.sem_inc(s_acc, 1)
            v.sem_inc(s_dacc, 1)
            v.memset(ps_seg[1][:, :], 0.0).then_inc(s_pz, 1)
            v.memset(ps_deg[0:1, 0:W], 0.0).then_inc(s_pz, 1)
            v.memset(brow[:, :], 0).then_inc(s_br, 1)

            def stats(b):
                v.wait_ge(s_x[b], 32)
                if b:
                    v.wait_ge(s_mv, BLK * b)
                for j in range(BLK):
                    v.bn_stats(st6[:, j, :], x_all[:, b * BLK + j, :]).then_inc(s_st, 1)
                if b:
                    v.wait_ge(s_r1, b)
                for j in range(BLK):
                    v.wait_ge(s_st, b * BLK + j + 1)
                    v.bn_aggr(mvs[:, j, :], st6[:, j, :]).then_inc(s_mv, 1)

            def low(b):
                o = (b % 2) * BLK
                v.wait_ge(s_hi16, b + 1)
                v.tensor_tensor(gring[0:TN, o:o + BLK, D:2 * D], x_all[:, b * BLK:(b + 1) * BLK, :], gring[0:TN, o:o + BLK, 0:D],
                                ALU.subtract).then_inc(s_lo16, 1)

            stats(0)
            stats(1)
            low(0)
            v.wait_ge(s_dst, 16)
            v.tensor_copy(rel[:, :], dst_i).then_inc(s_d, 1)
            v.wait_ge(s_d, 1)
            v.tensor_reduce(gmin[:, :], rel_g, AX, ALU.min).then_inc(s_d, 1)
            v.wait_ge(s_dp, 1)
            v.tensor_reduce(bcol[:, :], ps_t[0:NG, 0:P], AX, ALU.min).then_inc(s_d, 1)
            v.wait_ge(s_d, 3)
            v.tensor_scalar(bcol_w[:, :], ones[0:NG, :], bcol[:, 0:1], None, ALU.mult).then_inc(s_d, 1)
            v.wait_ge(s_dp, 2)
            v.tensor_copy(bwide[:, :], ps_y[:, 0:NG]).then_inc(s_d, 1)
            v.wait_ge(s_d, 5)
            v.tensor_tensor(rel_g, rel_g, wide(bwide[:, :], NG, GT), ALU.subtract).then_inc(s_d, 1)
            v.wait_ge(s_d, 6)
            v.scalar_tensor_tensor(rel_tmp, rel[:, :], MASKED / 10, rel[:, :], ALU.is_lt, ALU.mult).then_inc(s_d, 1)
            v.wait_ge(s_d, 7)
            v.tensor_reduce(okc[:, 0:1], rel_tmp, AX, ALU.max).then_inc(s_d, 1)
            v.wait_ge(s_dp, 3)
            v.tensor_reduce(okc[0:1, 1:2], ps_t[0:1, 0:P], AX, ALU.max).then_inc(s_d, 1)
            v.wait_ge(s_d, 9)
            v.tensor_scalar(okc[0:1, 2:3], okc[0:1, 1:2], float(W), None, ALU.is_lt).then_inc(s_d, 1)
            v.wait_ge(s_d, 10)
            v.tensor_copy(ok_i[:, :], okc[0:1, 2:3]).then_inc(s_d, 1)
            v.wait_ge(s_dp, 4)
            v.tensor_scalar(okc[:, 3:4], ps_xt[:, 0:1], -1.0, 1.0, ALU.mult, ALU.add).then_inc(s_d, 1)
            v.wait_ge(s_d, 12)
            v.tensor_scalar(gmin[:, :], bwide[:, :], okc[:, 3:4], None, ALU.mult).then_inc(s_d, 1)
            v.wait_ge(s_d, 13)
            v.tensor_tensor(rel_g, rel_g, wide(gmin[:, :], NG, GT), ALU.add).then_inc(s_d, 1)
            v.tensor_tensor(bwide[:, :], bwide[:, :], gmin[:, :], ALU.subtract).then_inc(s_d, 1)
            v.wait_ge(s_d, 15)
            v.wait_ge(s_br, 1)
            v.tensor_copy(brow[0:1, 1:NG + 1], bwide[0:1, :]).then_inc(s_rel, 1)
            v.wait_ge(s_iota, 1)
            v.tensor_copy(iota[:, :], iota_i[:, :]).then_inc(s_iota, 1)
            v.wait_ge(s_wkv, 16 * 6)
            wv = wstage[:, :, :].rearrange("p c (g e) -> p (c g) e", e=HC)
            v.tensor_reduce(wmean[:, :], wv, AX, ALU.add).then_inc(s_wprep, 1)
            v.wait_ge(s_wprep, 1)
            v.scalar_tensor_tensor(wv, wide(wmean[:, :], KC * GR, HC), -1.0 / HC, wv, ALU.mult, ALU.add).then_inc(s_wprep, 1)
            bv = bkv[:, :].rearrange("p (g e) -> p g e", e=HC)
            v.tensor_reduce(lnst[:, 0, :], bv, AX, ALU.add).then_inc(s_wprep, 1)
            v.wait_ge(s_wprep, 3)
            v.scalar_tensor_tensor(bv, wide(lnst[:, 0, :], GR, HC), -1.0 / HC, bv, ALU.mult, ALU.add).then_inc(s_wprep, 1)
            v.wait_ge(s_par, 16 * 11)
            v.tensor_tensor(brows[:, :], brows[:, :], hrows[:, :], ALU.add).then_inc(s_br, 1)
            for b in range(2, NT // BLK):
                stats(b)
                low(b - 1)
            low(NT // BLK - 1)
            v.wait_ge(s_wsplit, 1)
            v.tensor_tensor(wkv_lo[:, :, :], wstage[:, :, :], wkv_hi[:, :, :].bitcast(F32), ALU.subtract).then_inc(s_wsplit, 1)

            v.wait_ge(s_rel, 1)
            v.wait_ge(s_iota, 2)
            v.wait_ge(s_wprep, 4)
            v.wait_ge(s_br, 2)
            v.wait_ge(s_pz, 2)
            v.wait_ge(s_zero, 1 + NT // BLK)

            def one_hot(it, g, h):
                a, z = h * HT, (h + 1) * HT
                v.wait_ge(s_edge[h], fin(it, 1))
                v.wait_ge(s_hot16[h], fin(it, 1))
                v.tensor_tensor(s32[:, a:z, :], iota[:, :].unsqueeze(1).broadcast_to([P, HT, W]),
                                rel[:, ds(g * GT + a, HT)].unsqueeze(2).broadcast_to([P, HT, W]), ALU.is_equal).then_inc(s_hot[h], 1)

            def low_edges(it, h):
                a, z = h * HT, (h + 1) * HT
                v.wait_ge(s_ehi[h], fin(it))
                v.tensor_tensor(e_lo[:, a:z, :], e32[:, a:z, :], e_hi[:, a:z, :].bitcast(F32), ALU.subtract).then_inc(s_elo[h], 1)

            def degrees(it, g):
                b = v.value_load(brow[0:1, ds(g, 1)], min_val=0, max_val=NPAD - W)
                v.wait_ge(s_seg[1], fin(it, 1))
                v.wait_ge(s_dacc, fin(it, 2))
                v.tensor_tensor(deg_row[0:1, ds(b, W)], deg_row[0:1, ds(b, W)], ps_deg[0:1, 0:W], ALU.add).then_inc(s_dacc, 1)
                return b

            def flush(it, b):
                v.wait_ge(s_pj, fin(it, 1))
                v.wait_ge(s_acc, fin(it, 2))
                v.tensor_tensor(acc_y[:, :, ds(b, W)], acc_y[:, :, ds(b, W)], ps_y[:, 0:KC * W].rearrange("p (c n) -> p c n", c=KC),
                                ALU.add).then_inc(s_acc, 1)

            def body(it, u, pair, kv=None, mix=None, g=None, ahead=True, put=None):
                g = it if g is None else g
                one_hot(it, g, 1)
                low_edges(it, 1)
                b = degrees(it, g)
                if kv is not None:
                    v.wait_ge(s_xhi, fin(kv))
                    v.tensor_tensor(xt_lo[:, :, 0:TN], ps_xt[:, 0:KC * TN].rearrange("p (c n) -> p c n", c=KC),
                                    xt_hi[:, :, 0:TN].bitcast(F32), ALU.subtract).then_inc(s_xlo, 1)
                if mix is not None:
                    v.wait_ge(s_xhi, fin(mix + NT))
                    v.tensor_tensor(xt_lo[:, :, 0:CN], ps_xt[:, 0:KC * CN].rearrange("p (c n) -> p c n", c=KC),
                                    xt_hi[:, :, 0:CN].bitcast(F32), ALU.subtract).then_inc(s_xlo, 1)
                if ahead:
                    one_hot(it + 1, g + 1, 0)
                if kv is not None:
                    v.wait_ge(s_kvp, fin(kv))
                    v.wait_ge(s_sq, fin(kv, 1))
                    v.tensor_tensor(xc, ps_kv[0:TN, :], bkv[:, :], ALU.add).then_inc(s_xc, 1)
                if mix is not None:
                    v.wait_ge(s_hhi, fin(mix))
                    v.tensor_tensor(hm_lo[:, :, 0:CN], hm[:, :, 0:CN], hm_hi[:, :, 0:CN].bitcast(F32), ALU.subtract).then_inc(s_hlo, 1)
                if ahead:
                    low_edges(it + 1, 0)
                flush(it, b)
                if kv is not None:
                    kvg = kvn.rearrange("p (g e) -> p g e", e=HC)
                    kvh = kvn.rearrange("p (s h e) -> p s h e", s=2, e=HC)
                    v.wait_ge(s_sq, fin(kv))
                    v.tensor_reduce(lnst[:, 0, :], kvg, AX, ALU.add).then_inc(s_kd, 1)
                    v.wait_ge(s_kd, kv * 4 + 1)
                    v.tensor_scalar(lnst[:, 1, :], lnst[:, 0, :], 1.0 / HC, EPS, ALU.mult, ALU.add).then_inc(s_ve, 1)
                    v.wait_ge(s_sd, fin(kv))
                    v.reciprocal(lnst[:, 3, :], lnst[:, 2, :]).then_inc(s_kd, 1)
                    v.wait_ge(s_kd, kv * 4 + 2)
                    v.tensor_tensor(kvg, xc.rearrange("p (g e) -> p g e", e=HC), wide(lnst[:, 3, :], GR, HC), ALU.mult).then_inc(s_kd, 1)
                    v.wait_ge(s_kd, kv * 4 + 3)
                    v.tensor_tensor(kvh, kvh, lns[:, 0:2, :].unsqueeze(2).broadcast_to([TN, 2, HEADS, HC]), ALU.mult).then_inc(s_kd, 1)
                    v.wait_ge(s_kd, kv * 4 + 4)
                    v.tensor_tensor(kvh, kvh, lns[:, 2:4, :].unsqueeze(2).broadcast_to([TN, 2, HEADS, HC]), ALU.add).then_inc(s_kvn, 1)
                if mix is not None:
                    v.wait_ge(s_mst, mix * 2 + 2)
                    v.tensor_tensor(xch[:, u, :, :], xnc[:, :, :], xch[:, u, :, :], ALU.add).then_inc(s_b1, 1)
                    v.wait_ge(s_b1, mix * 2 + 1)
                    v.tensor_tensor(xch[:, u, :, :], xch[:, u, :, :], brows[:, :].unsqueeze(1).broadcast_to([TN, 2, D]), ALU.add).then_inc(s_b1, 1)
                    v.wait_ge(s_b1, mix * 2 + 2)
                    v.wait_ge(s_mp, fin(mix))
                    v.tensor_tensor(xch[:, u, :, :], xch[:, u, :, :], ps_acc[0:TN, :].rearrange("p (t d) -> p t d", t=2), ALU.add).then_inc(s_bs, 1)

            def between():
                v.wait_ge(s_kva, NT + 3)
                v.wait_ge(s_mask, 1 + P // HC)
                v.tensor_tensor(kv_t[:, :, :], ps_acc[:, 0:KC * P].rearrange("p (c n) -> p c n", c=KC),
                                block_mask[:, :].unsqueeze(1).broadcast_to([P, KC, P]), ALU.mult).then_inc(s_c, 1)
                v.wait_ge(s_cp, 1)
                v.tensor_copy(p_sb[:, :, :], ps_kv[:, :].rearrange("p (c n) -> p c n", c=KC)).then_inc(s_c, 1)
                v.wait_ge(s_cp, 2)
                v.tensor_tensor(p_sb[:, :, :], ps_xt[:, :].rearrange("p (c n) -> p c n", c=KC), w1_sb[:, :, :], ALU.add).then_inc(s_c, 1)
                v.tensor_tensor(bm[:, :], ps_acc[:, 0:KC], b1c[:, :], ALU.add).then_inc(s_c, 1)
                v.wait_ge(s_ca, 2)
                v.wait_ge(s_c, 3)
                v.tensor_tensor(m_lo[:, :, :], p_sb[:, :, :], m_hi[:, :, :].bitcast(F32), ALU.subtract).then_inc(s_c, 1)
                v.tensor_tensor(w2_lo[:, :, :], w2_sb, w2_hi[:, :, :].bitcast(F32), ALU.subtract).then_inc(s_c, 1)

            def start(k):
                for h in range(2):
                    v.wait_ge(s_hot[h], fin(k * NG, 1))
                v.tensor_scalar(rel[:, :], rel[:, :], -float(W), None, ALU.add).then_inc(s_pass, 1)
                v.tensor_copy(brow[0:1, 0:1], brow[0:1, NG:NG + 1]).then_inc(s_pass, 1)
                v.wait_ge(s_pass, k * 3 - 1)
                v.tensor_scalar(brow[0:1, 1:NG + 1], brow[0:1, 1:NG + 1], W, None, ALU.add).then_inc(s_pass, 1)
                v.wait_ge(s_pass, k * 3)
                v.sem_inc(s_carry_v, 1)
                first_half(k * NG)

            def first_half(it):
                one_hot(it, 0, 0)
                low_edges(it, 0)

            def epilogue(it):
                flush(it, degrees(it, NG))
                v.wait_ge(s_dacc, fin(it, 1))
                v.wait_ge(s_acc, fin(it, 1))
                v.sem_inc(s_sums, 1)

            first_half(0)
            schedule(v, body, between)
            general(v, body, start, epilogue)

            v.sem_inc(s_fx[0], 2)
            v.sem_inc(s_fx[1], 2)
            v.memset(zcol[:, :], 0.0).then_inc(s_nd, 1)
            v.wait_ge(s_np, 1)
            v.tensor_scalar(degs[:, 0, :], ps_t[0:TN, 0:NT], 1.0, None, ALU.max).then_inc(s_nd, 1)
            v.wait_ge(s_na, 1)
            v.reciprocal(degs[:, 2, :], degs[:, 1, :]).then_inc(s_nd, 1)
            v.wait_ge(s_nd, 3)
            v.scalar_tensor_tensor(norm[:, :], ps_t[0:TN, 0:NT], 0.0, degs[:, 2, :], ALU.is_gt, ALU.mult).then_inc(s_nd, 1)
            v.wait_ge(s_nd, 4)
            v.wait_ge(s_bl, 32 * (NT // BLK))

            def rows(c, u, i):
                v.wait_ge(s_ft[u], i + 2)
                for j in range(2):
                    t = c * 2 + j
                    v.scalar_tensor_tensor(x2[:, ds(t, 1), :], bank[u][0:TN, j * D:(j + 1) * D].unsqueeze(1), norm[:, ds(t, 1)],
                                           x2[:, ds(t, 1), :], ALU.mult, ALU.add).then_inc(s_fx[u], 1)
                for j in range(2):
                    v.wait_ge(s_fx[u], i * 2 + (j + 3))
                    v.sem_inc(s_carry_v, 1)
                    v.bn_stats(st6n[:, j, :], x2[:, ds(c * 2 + j, 1), :]).then_inc(s_fs, 1)
                for j in range(2):
                    v.wait_ge(s_fs, c * 4 + (j + 1))
                    wait_past(v, s_fv, c * 2)
                    v.sem_inc(s_carry_v, 1)
                    v.bn_aggr(mvn[:, j, :], st6n[:, j, :]).then_inc(s_fs, 1)
                v.wait_ge(s_fs, c * 4 + 4)
                v.wait_ge(s_r2, c * 2 + 2)
                v.tensor_scalar(ven[:, u, :], mvn[:, :, 1], EPS, None, ALU.add).then_inc(s_fv, 1)
                v.tensor_scalar(nmn[:, u, :], mvn[:, :, 0], -1.0, None, ALU.mult).then_inc(s_fv, 1)

            rows(0, 0, 0)
            with v.Fori(0, NC // 2) as i:
                for u in range(2):
                    rows(i * 2 + (1 + u), 1 - u, i + u)
            row = lambda n: rt[0:1, n, :]
            one = lambda n: rs[0:1, n:n + 1]
            v.wait_ge(s_r2, 2 * NC + 4)
            v.tensor_reduce(nsum[:, :], nmr2[:, :], AX, ALU.add).then_inc(s_rd, 1)
            v.wait_ge(s_rp, 1)
            v.tensor_copy(one(0), ps_t[0:1, 0:1]).then_inc(s_rd, 1)
            v.wait_ge(s_rd, 2)
            v.wait_ge(s_mean, NC)
            v.tensor_scalar(mrow[:, :], ps_kv[0:1, 0:D], one(0), 1.0 / N, ALU.add, ALU.mult).then_inc(s_rd, 1)
            v.wait_ge(s_rp, 2)
            v.tensor_copy(mean_c[:, :], ps_xt[:, 0:KC]).then_inc(s_rm, 1)
            v.wait_ge(s_rp, 3)
            v.wait_ge(s_rw, 32)
            v.tensor_tensor(row(1), ps_t[0:1, 0:EX], row(0), ALU.add).then_inc(s_rd, 1)
            v.wait_ge(s_rd, 4)
            v.tensor_reduce(one(1), row(1), AX, ALU.max, negate=True).then_inc(s_rd, 1)

            def softmax_rest(exps, total, inverse, result, n, m=EX):
                v.tensor_reduce(total, exps[:, 0:m], AX, ALU.add).then_inc(s_rd, 1)
                v.wait_ge(s_rd, n)
                v.reciprocal(inverse, total).then_inc(s_rd, 1)
                v.wait_ge(s_rd, n + 1)
                v.tensor_scalar(result[:, 0:m], exps[:, 0:m], inverse, None, ALU.mult).then_inc(s_rd, 1)
                v.wait_ge(s_rd, n + 2)

            v.wait_ge(s_ra, 1)
            softmax_rest(row(2), one(2), one(3), row(3), 6)
            v.tensor_scalar(row(4), row(3), float(N), None, ALU.mult).then_inc(s_rd, 1)
            v.wait_ge(s_rd, 9)
            v.tensor_scalar(row(5), row(4), CAPACITY, None, ALU.max).then_inc(s_rd, 1)
            v.wait_ge(s_rd, 10)
            v.reciprocal(row(6), row(5)).then_inc(s_rd, 1)
            v.wait_ge(s_rd, 11)
            v.tensor_scalar(row(6), row(6), CAPACITY, -1.0, ALU.mult, ALU.add).then_inc(s_rd, 1)
            v.wait_ge(s_rd, 12)
            v.scalar_tensor_tensor(row(7), row(4), CAPACITY, row(6), ALU.is_gt, ALU.mult).then_inc(s_rd, 1)
            v.wait_ge(s_rd, 13)
            v.tensor_scalar(row(7), row(7), 1.0, None, ALU.add).then_inc(s_rd, 1)
            v.wait_ge(s_rd, 14)
            v.tensor_tensor(row(8), row(3), row(7), ALU.mult).then_inc(s_rd, 1)
            v.wait_ge(s_rd, 15)
            v.tensor_reduce(one(5), row(8), AX, ALU.max, negate=True).then_inc(s_rd, 1)
            v.wait_ge(s_ra, 2)
            softmax_rest(row(9), one(6), one(7), row(10), 17)
            v.max(row(11), row(10)).then_inc(s_rd, 1)
            v.wait_ge(s_rd, 20)
            v.max_index(top_i[:, :], row(11), row(10)).then_inc(s_top, 1)
            v.tensor_scalar(one(8), rt[0:1, 11, 0:1], -1.0, None, ALU.mult).then_inc(s_rd, 1)
            v.wait_ge(s_ra, 3)
            softmax_rest(row(12), one(9), one(10), row(13), 22, 2)
            v.wait_ge(s_rd, 24)
            v.sem_inc(s_top, 1)

            v.wait_ge(s_bp, 1)
            v.tensor_copy(wts[:, :], ps_y[:, 0:2]).then_inc(s_wts, 1)
            v.wait_ge(s_wts, 1)
            v.memset(xf_hi[:, :, CN:CW].bitcast(F32), 0.0).then_inc(s_w1l, 1)
            v.memset(xf_lo[:, :, CN:CW].bitcast(F32), 0.0).then_inc(s_w1l, 1)
            for j in range(2):
                v.wait_ge(s_fw2[j], 16)
                v.tensor_scalar(fw2_st[:, j, :, :], fw2_st[:, j, :, :], wts[:, j:j + 1], None, ALU.mult).then_inc(s_w2s, 1)
            v.wait_ge(s_fb, 16 * 6)
            for j in range(2):
                v.tensor_scalar(fb2r[0:1, j, :], fb2r[0:1, j, :], wts[0:1, j:j + 1], None, ALU.mult).then_inc(s_w2s, 1)

            def rows_lo(c, u, i):
                v.wait_ge(s_xfh, c + 1)
                v.tensor_tensor(xf_lo[:, :, 0:CN], ps_xt[:, 0:KC * CN].rearrange("p (c n) -> p c n", c=KC), xf_hi[:, :, 0:CN].bitcast(F32),
                                ALU.subtract).then_inc(s_xfl, 1)

            def hidden(c, u, i):
                for q in range(FC // 2):
                    v.wait_ge(s_hh, c * (FC // 2) + (q + 1))
                    v.tensor_tensor(h_lo[:, u, 2 * q:2 * q + 2, :], h32[:, 2 * q:2 * q + 2, :], h_hi[:, u, 2 * q:2 * q + 2, :].bitcast(F32),
                                    ALU.subtract).then_inc(s_hl, 1)

            def added(c, u, i):
                v.wait_ge(s_g2[u], i + 1)
                v.wait_ge(s_xlb[u], i + 1)
                wait_past(v, s_rn[u], i * 2)
                v.tensor_tensor(o_sb[:, u, :, :], [ps_kv, ps_acc][u][0:TN, :].rearrange("p (t d) -> p t d", t=2), xlb[:, u, :, :],
                                ALU.add).then_inc(s_od[u], 1)
                v.wait_ge(s_od[u], i + 1)
                v.sem_inc(s_carry_v, 1)
                for j in range(2):
                    v.bn_stats(st6x[:, j, :], o_sb[:, u, j, :]).then_inc(s_xs, 1)
                for j in range(2):
                    v.wait_ge(s_xs, c * 4 + (j + 1))
                    wait_past(v, s_vx, c * 2)
                    v.sem_inc(s_carry_v, 1)
                    v.bn_aggr(mvx[:, j, :], st6x[:, j, :]).then_inc(s_xs, 1)
                v.wait_ge(s_xs, c * 4 + 4)
                v.tensor_scalar(vex[:, u, :], mvx[:, :, 1], EPS, None, ALU.add).then_inc(s_vx, 1)
                v.tensor_scalar(nmx[:, u, :], mvx[:, :, 0], -1.0, None, ALU.mult).then_inc(s_vx, 1)

            def finish(c, u, i):
                v.wait_ge(s_rn[u], i * 2 + 2)
                v.tensor_tensor(res[:, u, :, :], res[:, u, :, :], grow[:, :].unsqueeze(1).broadcast_to([TN, 2, D]), ALU.mult).then_inc(s_rg[u], 1)
                v.wait_ge(s_rg[u], i + 1)
                v.wait_ge(s_xb[u], i + 1)
                v.tensor_tensor(res[:, u, :, :], res[:, u, :, :], xb[:, u, :, :], ALU.add).then_inc(s_res[u], 1)

            def step(c, u, i):
                fixed = isinstance(c, int)
                if not (fixed and c + 1 >= NC):
                    hidden(c + 1, 1 - u, i + u)
                if not (fixed and c + 2 >= NC):
                    rows_lo(c + 2, u, i + 1)
                if not (fixed and c == 0):
                    finish(c - 1, 1 - u, i + (u - 1))
                added(c, u, i)

            v.wait_ge(s_bp, 2)
            v.tensor_copy(b2w[:, :], ps_acc[0:TN, 0:D]).then_inc(s_b2w, 1)
            for j in range(2):
                v.wait_ge(s_w1h, j + 1)
                v.tensor_tensor(fw1_lo[:, :, j * F:(j + 1) * F], fw1_st[:, j, :, :], fw1_hi[:, :, j * F:(j + 1) * F].bitcast(F32),
                                ALU.subtract).then_inc(s_w1l, 1)
            rows_lo(0, 0, 0)
            for j in range(2):
                v.wait_ge(s_w2h, j + 1)
                v.tensor_tensor(fw2_lo[:, j * (FC // 2):(j + 1) * (FC // 2), :], fw2_st[:, j, :, :],
                                fw2_hi[:, j * (FC // 2):(j + 1) * (FC // 2), :].bitcast(F32), ALU.subtract).then_inc(s_w2l, 1)
            hidden(0, 0, 0)
            rows_lo(1, 1, 0)
            chunks(v, step)
            finish(NC - 1, (NC - 1) % 2, NC // 2)


_ARGS = (("x", "x"), ("src_l", None), ("dst_l", None), ("edges", "edge_attr_256"), ("wgnn", "L0_gnn_weights"),
         ("hbias", "L0_gnn_h_bias"), ("w_qkv", "L0_mix_w_qkv"), ("wq_t", None), ("b_qkv", "L0_mix_b_qkv"), ("bq_l", None),
         ("kln_g", "L0_mix_kln_g"), ("kln_b", "L0_mix_kln_b"), ("vln_g", "L0_mix_vln_g"), ("vln_b", "L0_mix_vln_b"),
         ("w1", "L0_mix_w1"), ("b1_l", None), ("w2", "L0_mix_w2"), ("b2", "L0_mix_b2"), ("wr", "L0_ffn_Wr"),
         ("br", "L0_ffn_br"), ("fw1", "L0_ffn_W1"), ("fb1_l", None), ("fw2", "L0_ffn_W2"), ("fb2", "L0_ffn_b2"),
         ("gamma", "L0_ffn_gamma"), ("beta", "L0_ffn_beta"))


def kernel(**inputs):
    import numpy as np
    import concourse.bacc as bacc
    from concourse.bass_utils import run_bass_kernel_spmd

    starts = [g * GE for g in range(NG - 1)] + [LAST]
    edge_of = np.array(starts)[None, :, None] + np.arange(P)[:, None, None] * GT + np.arange(GT)[None, None, :]
    dst = np.ascontiguousarray(np.asarray(inputs["dst"])[edge_of])
    repeated = edge_of[:, -1, :] < (NG - 1) * GE
    dst[:, -1, :][repeated] = int(MASKED)
    src = np.asarray(inputs["src"])[edge_of]
    w_qkv = np.asarray(inputs["L0_mix_w_qkv"])
    wq_t = w_qkv.reshape(D, HEADS, 3, HC)[:, :, 0, :].reshape(D, D).T
    bq_l = np.asarray(inputs["L0_mix_b_qkv"]).reshape(HEADS, 3, HC)[:, 0, :].reshape(KC, P).T
    laid = {"src_l": src.reshape(P, -1), "dst_l": dst.reshape(P, -1), "wq_t": wq_t, "bq_l": bq_l,
            "b1_l": np.asarray(inputs["L0_mix_b1"]).reshape(KC, P).T,
            "fb1_l": np.asarray(inputs["L0_ffn_b1"]).reshape(EX, F // P, P).transpose(0, 2, 1)}

    nc = bacc.Bacc("TRN2", target_bir_lowering=False, num_devices=1)
    arrays, args = {}, []
    for name, source in _ARGS:
        a = np.ascontiguousarray(laid[name] if source is None else np.asarray(inputs[source]))
        arrays[name] = a
        args.append(nc.dram_tensor(name, a.shape, mybir.dt.from_np(a.dtype), kind="ExternalInput").ap())
    out = nc.dram_tensor("out", (N, D), F32, kind="ExternalOutput").ap()
    gps_layer(nc, *args, out)
    r = run_bass_kernel_spmd(nc, [arrays], core_ids=[0])
    return r.results[0]["out"]
```

```python
from contextlib import ExitStack

import concourse.bass as bass
from concourse import mybir

ALU = mybir.AluOpType
ACT = mybir.ActivationFunctionType
AX = mybir.AxisListType.X
F32 = mybir.dt.float32
F32R = mybir.dt.float32r
F16 = mybir.dt.float16
I32 = mybir.dt.int32
U32 = mybir.dt.uint32
ds = bass.ds

P = 128
N = 6250
D = 256
E = 106250
KC = D // P
TN = 125
NT = N // TN
CN = 2 * TN
NC = NT // 2
CW = 256
GT = 10
HT = GT // 2
GE = P * GT
NG = -(-E // GE)
LAST = E - P
assert E - (NG - 1) * GE <= P
W = 128
PASSES = -(-N // W)
NPAD = PASSES * W + W
HEADS = 8
HC = D // HEADS
GR = 2 * HEADS
EX = 8
F = 512
FC = 2 * F // P
EPS = 1e-5
CAPACITY = float(-(-N * 5 // (4 * EX)))
BLK = 10
BLK_POOL = 2
GAP = 12000
MASKED = 1.0e6


def fin(it, back=0):
    return it + 3 - back


def wait_past(eng, semaphore, value):
    if not (isinstance(value, int) and value <= 0):
        eng.wait_ge(semaphore, value)


def gps_layer(nc, x, src_l, dst_l, edges, wgnn, hbias, w_qkv, wq_t, b_qkv, bq_l, kln_g, kln_b, vln_g, vln_b,
              w1, b1_l, w2, b2, wr, br, fw1, fb1_l, fw2, fb2, gamma, beta, out):
    ctx = ExitStack()
    with ctx:
        def alloc(stack):
            return lambda name, shape, dt=F32: stack.enter_context(nc.sbuf_tensor(name, shape, dt))

        def sem(name):
            return ctx.enter_context(nc.semaphore(name))

        table = nc.dram_tensor("xn_table", [N, 2 * D], F16, kind="Internal").ap()
        base_d = nc.dram_tensor("base_rows", [CN + N, D], F32, kind="Internal").ap()
        deg_d = nc.dram_tensor("deg_row", [1, N], F32, kind="Internal").ap()

        sb = alloc(ctx)
        ident = sb("ident", [P, P])
        ones = sb("ones", [P, P])
        r1 = sb("r1", [TN, NT])
        nmr1 = sb("nmr1", [TN, NT])
        r2 = sb("r2", [TN, NT])
        nmr2 = sb("nmr2", [TN, NT])
        norm = sb("norm", [TN, NT])
        half = sb("half", [TN, BLK])
        ok_i = sb("ok_i", [1, 1], I32)

        sums = ExitStack()
        sbs = alloc(sums)
        acc_y = sbs("acc_y", [P, KC, NPAD])
        deg_row = sbs("deg_row_sb", [1, NPAD])
        edge_phase = ExitStack()
        sbe = alloc(edge_phase)
        gring = sbe("gring", [P, 2 * GT, 2 * D], F16)
        e32 = sbe("e32", [P, GT, D])
        e_hi = sbe("e_hi", [P, GT, D], F32R)
        e_lo = sbe("e_lo", [P, GT, D], F32R)
        s32 = sbe("s32", [P, GT, W], F32R)
        s16 = sbe("s16", [P, GT, W], F16)
        ones16 = sbe("ones16", [P, 1], F16)
        iota = sbe("iota", [P, W])
        iota_i = sbe("iota_i", [P, W], I32)
        rel = sbe("rel", [P, NG * GT])
        src_sb = sbe("src_sb", [P, NG * GT], I32)
        idx = sbe("idx", [P, 2 * GT], I32)
        gmin = sbe("gmin", [P, NG])
        bcol = sbe("bcol", [NG, 1])
        bcol_w = sbe("bcol_w", [NG, P])
        bwide = sbe("bwide", [P, NG])
        brow = sbe("brow", [1, NG + 1], I32)
        okc = sbe("okc", [P, 4])
        fl = sbe("fl", [P, D])
        fl_t = sbe("fl_t", [P, 4, W])
        wg = sbe("wg", [P, 4, D])
        wkv_hi = sbe("wkv_hi", [P, KC, 2 * D], F32R)
        wkv_lo = sbe("wkv_lo", [P, KC, 2 * D], F32R)
        bkv = sbe("bkv", [TN, 2 * D])
        lns = sbe("lns", [TN, 4, HC])
        m_hi = sbe("m_hi", [P, KC, D], F32R)
        m_lo = sbe("m_lo", [P, KC, D], F32R)
        w2_hi = sbe("w2_hi", [P, KC, D], F32R)
        w2_lo = sbe("w2_lo", [P, KC, D], F32R)
        wq_sb = sbe("wq_sb", [P, KC, D])
        w1_sb = sbe("w1_sb", [P, KC, D])
        p_sb = sbe("p_sb", [P, KC, D])
        bq = sbe("bq", [P, KC])
        b1c = sbe("b1c", [P, KC])
        bm = sbe("bm", [P, KC])
        brows = sbe("brows", [TN, D])
        hrows = sbe("hrows", [TN, D])
        block_mask = sbe("block_mask", [P, P])
        kv_t = sbe("kv_t", [P, KC, P])
        xch = sbe("xch", [TN, 2, 2, D])
        xnc = sbe("xnc", [TN, 2, D])
        xt_hi = sbe("xt_hi", [P, KC, CW], F32R)
        xt_lo = sbe("xt_lo", [P, KC, CW], F32R)
        work = sbe("work", [TN, 2, 2 * D])
        xc, kvn = (work[:, j, :] for j in range(2))
        lnst = sbe("lnst", [TN, 4, GR])
        hm_hi = sbe("hm_hi", [P, KC, CW], F32R)
        hm_lo = sbe("hm_lo", [P, KC, CW], F32R)
        st6 = sbe("st6", [TN, BLK, 6])
        mvs = sbe("mvs", [TN, BLK, 2])
        ve = sbe("ve", [TN, BLK])
        nm = sbe("nm", [TN, BLK])
        wstage = sbe("wstage", [P, KC, 2 * D])
        tab_in = sbe("tab_in", [1, 3])
        wmean = sbe("wmean", [P, KC * GR])
        w2_sb = wstage[:, :, 0:D]
        hm = wstage[:, :, D:D + CW]
        edge_phase.close()
        node_phase = ExitStack()
        sbn = alloc(node_phase)
        y_st = sbn("y_st", [P, 2, KC, CN])
        y_n = sbn("y_n", [TN, 2, 2, D])
        st6n = sbn("st6n", [TN, 2, 6])
        mvn = sbn("mvn", [TN, 2, 2])
        ven = sbn("ven", [TN, 2, 2])
        nmn = sbn("nmn", [TN, 2, 2])
        rst = sbn("rst", [TN, 2, 2])
        sdn = sbn("sdn", [TN, 2, 2])
        zcol = sbn("zcol", [P, 1])
        nsum = sbn("nsum", [TN, 1])
        mrow = sbn("mrow", [1, D])
        deg_t = sbn("deg_t", [NT, TN])
        degs = sbn("degs", [TN, 3, NT])
        wr_sb = sbn("wr_sb", [P, KC, EX])
        mean_c = sbn("mean_c", [P, KC])
        rt = sbn("rt", [1, 16, EX])
        rs = sbn("rs", [1, 16])
        top_i = sbn("top_i", [1, EX], U32)
        gap = sbn("gap", [P, GAP])
        x2 = sbn("x2", [TN, NT, D])
        node_phase.close()
        sums.close()
        sbx = alloc(ctx)
        fw1_st = sbx("fw1_st", [P, 2, KC, F])
        fw2_st = sbx("fw2_st", [P, 2, FC // 2, D])
        fw1_hi = sbx("fw1_hi", [P, KC, 2 * F], F32R)
        fw1_lo = sbx("fw1_lo", [P, KC, 2 * F], F32R)
        fw2_hi = sbx("fw2_hi", [P, FC, D], F32R)
        fw2_lo = sbx("fw2_lo", [P, FC, D], F32R)
        fb1c = sbx("fb1c", [P, FC])
        fb2r = sbx("fb2r", [1, 2, D])
        grow = sbx("grow", [TN, D])
        berow = sbx("berow", [TN, D])
        b2w = sbx("b2w", [TN, D])
        wts = sbx("wts", [P, 2])
        xl = sbx("xl", [TN, 2, 2, D])
        xf_hi = sbx("xf_hi", [P, KC, CW], F32R)
        xf_lo = sbx("xf_lo", [P, KC, CW], F32R)
        h32 = sbx("h32", [P, FC, CW])
        h_hi = sbx("h_hi", [P, 2, FC, CW], F32R)
        h_lo = sbx("h_lo", [P, 2, FC, CW], F32R)
        xlb = sbx("xlb", [TN, 2, 2, D])
        xb = sbx("xb", [TN, 2, 2, D])
        o_sb = sbx("o_sb", [TN, 2, 2, D])
        res = sbx("res", [TN, 2, 2, D])
        st6x = sbx("st6x", [TN, 2, 6])
        mvx = sbx("mvx", [TN, 2, 2])
        vex = sbx("vex", [TN, 2, 2])
        nmx = sbx("nmx", [TN, 2, 2])
        rx = sbx("rx", [TN, 2, 2])
        bnx = sbx("bnx", [TN, 2, 2])

        bank = [ctx.enter_context(nc.psum_tensor(f"bank{b}", [P, 512], F32)) for b in range(8)]
        ps_seg = [bank[0], bank[1]]
        ps_t, ps_y, ps_deg, ps_xt, ps_kv, ps_acc = bank[2:8]

        x_all = acc_y[0:TN, :, :].rearrange("p c n -> p (c n)").rearrange("p (t d) -> p t d", d=D)
        zero_blk = acc_y[:, :, :].rearrange("p c n -> p (c n)").rearrange("p (b n) -> p b n", b=NT // BLK)
        dst_i = e32[:, :, :].rearrange("p k d -> p (k d)")[:, 0:NG * GT].bitcast(I32)
        rel_tmp = e32[:, :, :].rearrange("p k d -> p (k d)")[:, NG * GT:2 * NG * GT]
        rel_g = rel[:, :].rearrange("p (g k) -> p g k", k=GT)
        slots = [range(0, HT), range(HT, GT)]
        ALL, SHORT = range(GT), (0, HT)

        def wide(ap, n, m):
            return ap.unsqueeze(2).broadcast_to([ap.shape[0], n, m])

        s_dst, s_src, s_wkv, s_par, s_w2 = (sem(f"s_{n}") for n in ("dst", "src", "wkv", "par", "w2"))
        s_x = [sem(f"s_x{b}") for b in range(NT // BLK)]
        s_st, s_mv, s_ps, s_r1, s_xn, s_xnp, s_hi16, s_lo16, s_zero = (sem(f"s_{n}") for n in (
            "st", "mv", "ps", "r1", "xn", "xnp", "hi16", "lo16", "zero"))
        s_tab = [sem(f"s_tab{b}") for b in range(2)]
        s_id, s_const, s_iota, s_mask, s_d, s_dp, s_rel, s_wprep, s_wsplit = (sem(f"s_{n}") for n in (
            "id", "const", "iota", "mask", "d", "dp", "rel", "wprep", "wsplit"))
        s_e = [[sem(f"s_e{u}{h}") for h in range(2)] for u in range(2)]
        s_gat = [[sem(f"s_gat{u}{h}") for h in range(2)] for u in range(2)]
        s_idx, s_carry, s_fl, s_flx, s_tp, s_flt, s_pj, s_acc, s_dacc = (sem(f"s_{n}") for n in (
            "idx", "carry", "fl", "flx", "tp", "flt", "pj", "acc", "dacc"))
        s_hot, s_ehi, s_hot16, s_elo, s_edge, s_seg = ([sem(f"s_{n}{h}") for h in range(2)] for n in (
            "hot", "ehi", "hot16", "elo", "edge", "seg"))
        s_xl = [sem(f"s_xl{u}") for u in range(2)]
        s_xst, s_xt, s_xhi, s_xlo, s_kvp, s_xc, s_sq, s_ve, s_sd, s_kd, s_kvn, s_kva = (
            sem(f"s_{n}") for n in ("xst", "xt", "xhi", "xlo", "kvp", "xc", "sq", "ve", "sd", "kd", "kvn",
                                    "kva"))
        s_c, s_ca, s_cp = (sem(f"s_{n}") for n in ("c", "ca", "cp"))
        s_bd = [sem(f"s_bd{u}") for u in range(2)]
        s_hp, s_hg, s_hhi, s_hlo, s_mp, s_b1, s_bs = (
            sem(f"s_{n}") for n in ("hp", "hg", "hhi", "hlo", "mp", "b1", "bs"))
        s_pass, s_sums, s_pz, s_br = (sem(f"s_{n}") for n in ("pass", "sums", "pz", "br"))
        s_dg, s_rw, s_np, s_na, s_nd, s_y, s_fs, s_fv, s_sdn, s_rst, s_r2, s_mean, s_kept = (
            sem(f"s_{n}") for n in ("dg", "rw", "np", "na", "nd", "y", "fs", "fv", "sdn", "rst", "r2", "mean", "kept"))
        s_bl, s_ft, s_fz, s_fx = ([sem(f"s_{n}{u}") for u in range(2)] for n in ("bl", "ft", "fz", "fx"))
        s_rd, s_rp, s_ra, s_rm, s_top = (sem(f"s_{n}") for n in ("rd", "rp", "ra", "rm", "top"))
        s_fw1, s_fw2 = ([sem(f"s_{n}{j}") for j in range(2)] for n in ("fw1", "fw2"))
        s_fb, s_b2w, s_w1h, s_w1l, s_w2s, s_w2h, s_w2l, s_bp = (sem(f"s_{n}") for n in (
            "fb", "b2w", "w1h", "w1l", "w2s", "w2h", "w2l", "bp"))
        s_xl2, s_xtp, s_xlb, s_xb, s_g2, s_od, s_rn, s_rg, s_res, s_out = ([sem(f"s_{n}{u}") for u in range(2)] for n in (
            "xl2", "xtp", "xlb", "xb", "g2", "od", "rn", "rg", "res", "out"))
        s_xfh, s_xfl, s_g1, s_ge, s_hh, s_hl, s_xs, s_vx, s_rx, s_bnx = (sem(f"s_{n}") for n in (
            "xfh", "xfl", "g1", "ge", "hh", "hl", "xs", "vx", "rx", "bnx"))

        block = ctx.enter_context(nc.Block())
        PAIRS_KV, PAIRS_MIX, PAIRS_REST = NT // 2, NC // 2, (NG - NT - 2 * (NC // 2) - 4) // 2
        G_MIX = NT + 2
        G_ODD = G_MIX + 2 * PAIRS_MIX
        G_REST = G_ODD + 2

        def schedule(eng, body, between, last=None):
            with eng.Fori(0, PAIRS_KV) as i:
                for u in range(2):
                    body(i * 2 + u, u, i, kv=i * 2 + u)
            between(0)
            for u in range(2):
                body(NT + u, u, NT // 2, fold=1 + u)
                between(1 + u)
            with eng.Fori(0, PAIRS_MIX) as i:
                for u in range(2):
                    body(i * 2 + (G_MIX + u), u, i + G_MIX // 2, mix=i * 2 + u)
            body(G_ODD, 0, G_ODD // 2, mix=NC - 1)
            body(G_ODD + 1, 1, G_ODD // 2, put=NC - 1)
            with eng.Fori(0, PAIRS_REST - 1) as i:
                for u in range(2):
                    body(i * 2 + (G_REST + u), u, i + G_REST // 2)
            for u in range(2):
                (last or body)(NG - 2 + u, u, NG // 2 - 1, ahead=u == 0)

        def general(eng, body, start=None, epilogue=None, last=None):
            eng.wait_ge(s_rel, 1)
            ok = eng.value_load(ok_i[0:1, 0:1], min_val=0, max_val=1)
            with eng.If(ok < 1):
                with eng.Fori(1, PASSES) as k:
                    if start is not None:
                        start(k)
                    with eng.Fori(0, NG // 2 - 1) as i:
                        for u in range(2):
                            body(k * NG + (i * 2 + u), u, k * (NG // 2) + i, g=i * 2 + u, lap=k, i=i)
                    for u in range(2):
                        (last or body)(k * NG + (NG - 2 + u), u, k * (NG // 2) + (NG // 2 - 1), g=NG - 2 + u, ahead=u == 0, lap=k, i=NG // 2 - 1)
                if epilogue is not None:
                    epilogue(NG * PASSES)
            if epilogue is not None:
                with eng.Else():
                    epilogue(NG)

        def node_chunks(eng, step):
            with eng.Fori(0, NC // 2 - 2) as i:
                for u in range(2):
                    step(i * 2 + u, u, i)
            for c in range(NC - 5, NC):
                step(c, c % 2, c // 2)

        def chunks(eng, step):
            for c in range(2):
                step(c, c, 0)
            with eng.Fori(1, NC // 2 - 1) as i:
                for u in range(2):
                    step(i * 2 + u, u, i)
            for c in range(NC - 3, NC):
                step(c, c % 2, c // 2)

        @block.sync
        def _(sp):
            sp.dma_start(e32[:, :, :].rearrange("p k d -> p (k d)")[:, 0:NG * GT].bitcast(I32), dst_l).then_inc(s_dst, 16)
            for b in range(NT // BLK):
                rows = x[b * BLK * TN:(b + 1) * BLK * TN, :].rearrange("(t p) d -> p t d", p=TN)
                for a, z in ((0, 112), (112, TN)):
                    sp.dma_start(x_all[a:z, b * BLK:(b + 1) * BLK, :], rows[a:z]).then_inc(s_x[b], 16)
            sp.dma_start(src_sb[:, :], src_l).then_inc(s_src, 16)
            for c in range(KC):
                for j in range(2):
                    sp.dma_start(wstage[:, c, j * D:(j + 1) * D].rearrange("p (h e) -> p h e", e=HC),
                                 w_qkv[c * P:(c + 1) * P, :].rearrange("p (h s e) -> p h s e", s=3, e=HC)[:, :, j + 1, :]
                                 ).then_inc(s_wkv, 16)
            for j in range(2):
                sp.dma_start(bkv[:, j * D:(j + 1) * D].rearrange("p (h e) -> p h e", e=HC),
                             b_qkv.rearrange("(h s e) -> h s e", s=3, e=HC)[:, j + 1, :].partition_broadcast(TN)
                             ).then_inc(s_wkv, 16)
            for j, row in enumerate((kln_g, vln_g, kln_b, vln_b)):
                sp.dma_start(lns[:, j, :], row.partition_broadcast(TN)).then_inc(s_par, 16)
            sp.dma_start(wg[:, :, :], wgnn.rearrange("(c p) d -> p c d", p=P)).then_inc(s_par, 16)
            sp.dma_start(wq_sb[:, :, :], wq_t.rearrange("(c p) d -> p c d", p=P)).then_inc(s_par, 16)
            sp.dma_start(bq[:, :], bq_l).then_inc(s_par, 16)
            sp.dma_start(w1_sb[:, :, :], w1.rearrange("(c p) d -> p c d", p=P)).then_inc(s_par, 16)
            sp.dma_start(b1c[:, :], b1_l).then_inc(s_par, 16)
            sp.dma_start(brows[:, :], b2.partition_broadcast(TN)).then_inc(s_par, 16)
            sp.dma_start(hrows[:, :], hbias.partition_broadcast(TN)).then_inc(s_par, 16)
            for b in range(NT // BLK):
                rows = table[b * BLK * TN:(b + 1) * BLK * TN, :].rearrange("(t p) d -> p t d", p=TN)
                o = (b % 2) * BLK
                for part, ready in ((slice(0, D), s_hi16), (slice(D, 2 * D), s_lo16)):
                    sp.wait_ge(ready, b + 1)
                    for a, z in ((0, 112), (112, TN)):
                        sp.dma_start(rows[a:z, :, part], gring[a:z, o:o + BLK, part]).then_inc(s_tab[b % 2], 16)
            sp.wait_ge(s_wsplit, 2)
            sp.dma_start(w2_sb, w2.rearrange("(c p) d -> p c d", p=P)).then_inc(s_w2, 16)
            sp.wait_ge(s_rel, 1)

            def load_group(it, u, pair, start, kv, mix):
                rows = edges[ds(start, GE), :].rearrange("(p k) d -> p k d", k=GT)
                if kv is not None:
                    xr = x[ds(kv * TN, TN), :]
                if mix is not None:
                    xr = x[ds(mix * CN, CN), :].rearrange("(t p) d -> p t d", p=TN)
                for h in range(2):
                    part = rows[:, h * HT:(h + 1) * HT, :]
                    sp.wait_ge(s_elo[h], fin(it, 1))
                    sp.dma_start(e32[:, h * HT:(h + 1) * HT, :], part).then_inc(s_e[u][h], 16)
                if kv is not None:
                    sp.wait_ge(s_xst, fin(kv, 2))
                    sp.dma_start(xch[:, u, 0, :], xr).then_inc(s_xl[u], 16)
                if mix is not None:
                    sp.wait_ge(s_bd[u], (pair + (1 - G_MIX // 2)) * 16)
                    sp.dma_start(xch[:, u, :, :], xr).then_inc(s_xl[u], 16)

            def body(it, u, pair, kv=None, mix=None, g=None, ahead=True, put=None, lap=0, i=None, fold=None):
                load_group(it, u, pair, (it if g is None else g) * GE, kv, mix)

            def last(it, u, pair, g=None, ahead=True, lap=0, i=None):
                if u == 0:
                    load_group(it, u, pair, (NG - 2) * GE, None, None)
                    return
                for h in range(2):
                    sp.wait_ge(s_elo[h], fin(it, 1))
                    sp.dma_start(e32[:, h * HT, :], edges[LAST:LAST + P, :]).then_inc(s_e[u][h], 16)

            def between(step):
                if step == 2:
                    sp.wait_ge(s_xst, NT + 2)

            schedule(sp, body, between, last)
            general(sp, body, last=last)

            sp.wait_ge(s_sums, 1)
            sp.dma_start(deg_d, deg_row[0:1, 0:N]).then_inc(s_dg, 16)
            sp.wait_ge(s_dg, 16)
            sp.dma_start(deg_t[:, :], deg_d.rearrange("o (t p) -> (o t) p", p=TN)).then_inc(s_dg, 16)
            sp.wait_ge(s_bd[0], 16 * (NC - NC // 2 + 1))
            sp.wait_ge(s_bd[1], 16 * (NC // 2 + 1))
            def fetch(c, u, i):
                rows = base_d[ds(c * CN + CN, CN), :].rearrange("(t p) d -> p t d", p=TN)
                wait_past(sp, s_bl[u], i * 32)
                for a, z in ((0, 112), (112, TN)):
                    sp.dma_start(x2[a:z, ds(c * 2, 2), :], rows[a:z]).then_inc(s_bl[u], 16)

            fetch(0, 0, 0)
            fetch(1, 1, 0)
            with sp.Fori(1, NC // 2) as i:
                for u in range(2):
                    fetch(i * 2 + u, u, i)
            fetch(NC - 1, 0, NC // 2)
            sp.dma_start(wr_sb[:, :, :], wr.rearrange("(c p) e -> p c e", p=P)).then_inc(s_rw, 16)
            sp.dma_start(rt[0:1, 0, :], br.partition_broadcast(1)).then_inc(s_rw, 16)
            sp.wait_ge(s_top, 1)
            chosen = [sp.value_load(top_i[0:1, j:j + 1], min_val=0, max_val=EX - 1) for j in range(2)]
            for j, e in enumerate(chosen):
                sp.dma_start(fw1_st[:, j, :, :], fw1[ds(e, 1), :, :].rearrange("e (c p) f -> p (e c) f", p=P)).then_inc(s_fw1[j], 16)
            for j, e in enumerate(chosen):
                sp.dma_start(fb1c[:, j * (FC // 2):(j + 1) * (FC // 2)],
                             fb1_l[ds(e, 1), :, :].rearrange("e p f -> p (e f)")).then_inc(s_fb, 16)
                sp.dma_start(fb2r[0:1, j, :], fb2[ds(e, 1), :]).then_inc(s_fb, 16)
            for j, e in enumerate(chosen):
                sp.dma_start(fw2_st[:, j, :, :], fw2[ds(e, 1), :, :].rearrange("e (f p) d -> p (e f) d", p=P)).then_inc(s_fw2[j], 16)
            sp.dma_start(grow[:, :], gamma.partition_broadcast(TN)).then_inc(s_fb, 16)
            sp.dma_start(berow[:, :], beta.partition_broadcast(TN)).then_inc(s_fb, 16)

            def store(c, u, i):
                rows = out[ds(c * CN, CN), :].rearrange("(t p) d -> p t d", p=TN)
                sp.wait_ge(s_res[u], i + 1)
                sp.dma_start(rows, res[:, u, :, :]).then_inc(s_out[u], 16)

            with sp.Fori(0, NC // 2) as i:
                for u in range(2):
                    store(i * 2 + u, u, i)
            store(NC - 1, 0, NC // 2)
            sp.wait_ge(s_out[0], 16 * (NC - NC // 2))
            sp.wait_ge(s_out[1], 16 * (NC // 2))

        @block.gpsimd
        def _(pool):
            pool.memset(ident[:, :], 0.0).then_inc(s_id, 1)
            pool.memset(ones[:, :], 1.0).then_inc(s_const, 1)
            pool.wait_ge(s_id, 1)
            pool.affine_select(out=ident[:, :], in_=ident[:, :], compare_op=ALU.not_equal, fill=1.0, base=0,
                               pattern=[[-1, P]], channel_multiplier=1).then_inc(s_id, 1)
            pool.memset(ones16[:, :], 1.0).then_inc(s_const, 1)
            pool.memset(half[:, :], -0.5).then_inc(s_const, 1)
            pool.memset(xch[:, 1, 1, :], 0.0).then_inc(s_const, 1)
            pool.memset(tab_in[:, :], 1.0).then_inc(s_const, 1)
            pool.iota(iota_i[:, :], [[1, W]], base=0, channel_multiplier=0).then_inc(s_iota, 1)
            pool.memset(block_mask[:, :], 0.0).then_inc(s_mask, 1)
            pool.wait_ge(s_mask, 1)
            for j in range(P // HC):
                pool.memset(block_mask[j * HC:(j + 1) * HC, j * HC:(j + 1) * HC], 1.0 / N).then_inc(s_mask, 1)
            pool.wait_ge(s_mask, 1 + P // HC)
            pool.memset(kvn, 0.0).then_inc(s_const, 1)
            for t in (xt_hi, xt_lo, hm_hi, hm_lo):
                pool.memset(t[:, :, :].bitcast(F32), 0.0).then_inc(s_const, 1)
            pool.memset(deg_row[:, :], 0.0).then_inc(s_zero, 1)

            def small(b):
                pool.wait_ge(s_mv, BLK * (b + 1))
                pool.tensor_scalar(ve[:, :], mvs[:, :, 1], EPS, None, ALU.add).then_inc(s_ps, 1)
                if b:
                    pool.wait_ge(s_r1, b)
                pool.tensor_scalar(nm[:, :], mvs[:, :, 0], -1.0, None, ALU.mult).then_inc(s_ps, 1)
                pool.wait_ge(s_ps, 3 * b + 2)
                pool.tensor_tensor(r1[:, ds(b * BLK, BLK)], ve[:, :], half[:, :], ALU.pow).then_inc(s_ps, 1)
                pool.wait_ge(s_ps, 3 * b + 3)
                pool.tensor_tensor(nmr1[:, ds(b * BLK, BLK)], nm[:, :], r1[:, ds(b * BLK, BLK)],
                                   ALU.mult).then_inc(s_r1, 1)

            def zero(b):
                pool.wait_ge(s_lo16, b + 1)
                pool.memset(zero_blk[:, ds(b, 1), :] if not isinstance(b, int) else zero_blk[:, b:b + 1, :],
                            0.0).then_inc(s_zero, 1)

            pool.wait_ge(s_const, 10)
            for b in range(NT // BLK):
                small(b)
                pool.wait_ge(s_r1, b + 1)
                for t in range((b + 1) * BLK - BLK_POOL, (b + 1) * BLK):
                    pool.tensor_scalar(x_all[:, t, :], x_all[:, t, :], r1[:, t:t + 1], nmr1[:, t:t + 1], ALU.mult, ALU.add).then_inc(s_xnp, 1)
            for b in range(NT // BLK):
                zero(b)
            for b in range(NT // BLK):
                pool.wait_ge(s_tab[b % 2], 64 * (b // 2 + 1))

            def gather(u, k):
                pool.indirect_dma_start(
                    out=gring[:, k, :], out_offset=None, in_=table,
                    in_offset=bass.IndirectOffsetOnAxis(ap=idx[:, k:k + 1], axis=0),
                ).then_inc(s_gat[u][k % GT // HT], 16)

            def body(it, u, pair, kv=None, mix=None, g=None, ahead=True, put=None, lap=0, i=None, fold=None):
                pool.wait_ge(s_idx, fin(it))
                pool.sem_inc(s_carry, 1)
                for k in range(u * GT, (u + 1) * GT):
                    gather(u, k)

            def last(it, u, pair, g=None, ahead=True, lap=0, i=None):
                if u == 0:
                    body(it, u, pair, g=g)
                    return
                pool.wait_ge(s_idx, fin(it))
                pool.sem_inc(s_carry, 1)
                for k in SHORT:
                    gather(u, u * GT + k)

            with pool.Fori(0, NG // 2 - 1) as i:
                for u in range(2):
                    body(i * 2 + u, u, i)
            for u in range(2):
                last(NG - 2 + u, u, NG // 2 - 1)
            general(pool, body, last=last)

            pool.sem_inc(s_fx[0], 1)
            pool.sem_inc(s_fx[1], 1)
            pool.wait_ge(s_sums, 1)

            def add(c, u, i):
                pool.wait_ge(s_bl[u], i * 32 + 32)
                pool.wait_ge(s_fz[u], i * 2 + 4)
                pool.tensor_tensor(y_n[:, u, :, :], x2[:, ds(c * 2, 2), :], y_n[:, u, :, :], ALU.add).then_inc(s_fx[u], 1)

            node_chunks(pool, add)

            pool.wait_ge(s_top, 1)
            pool.wait_ge(s_b2w, 1)
            pool.wait_ge(s_fb, 16 * 6)

            def residual(c, u, i):
                pool.wait_ge(s_xl2[u], i * 2 + 2)
                wait_past(pool, s_od[u], i)
                pool.tensor_tensor(xlb[:, u, :, :], xl[:, u, :, :], b2w[:, :].unsqueeze(1).broadcast_to([TN, 2, D]),
                                   ALU.add).then_inc(s_xlb[u], 1)

            def step(c, u, i):
                if not (isinstance(c, int) and c + 1 >= NC):
                    residual(c + 1, 1 - u, i + u)
                wait_past(pool, s_res[u], i)
                pool.tensor_tensor(xb[:, u, :, :], x2[:, ds(c * 2, 2), :], berow[:, :].unsqueeze(1).broadcast_to([TN, 2, D]),
                                   ALU.add).then_inc(s_xb[u], 1)
                pool.wait_ge(s_vx, c * 2 + 2)
                wait_past(pool, s_bnx, c)
                pool.tensor_tensor(rx[:, u, :], vex[:, u, :], half[:, 0:2], ALU.pow).then_inc(s_rx, 1)
                pool.wait_ge(s_rx, c + 1)
                pool.tensor_tensor(bnx[:, u, :], nmx[:, u, :], rx[:, u, :], ALU.mult).then_inc(s_bnx, 1)

            residual(0, 0, 0)
            chunks(pool, step)

        @block.scalar
        def _(act):
            def copy(o, i):
                return nc.scalar.activation(o, i, ACT.Copy)

            act.sem_inc(s_ehi[0], 2)
            act.sem_inc(s_ehi[1], 2)
            act.sem_inc(s_hot16[0], 2)
            act.sem_inc(s_hot16[1], 2)
            act.sem_inc(s_fl, 1)
            act.sem_inc(s_flt, 1)
            act.sem_inc(s_flx, 1)
            act.sem_inc(s_bd[0], 16)
            for s in (s_xst, s_xhi, s_sq, s_sd, s_hg, s_hhi):
                act.sem_inc(s, 2)
            for b in range(NT // BLK):
                act.wait_ge(s_r1, b + 1)
                for j in range(BLK - BLK_POOL):
                    t = b * BLK + j
                    nc.scalar.activation(x_all[:, t, :], x_all[:, t, :], ACT.Identity, bias=nmr1[:, t:t + 1],
                                         scale=r1[:, t:t + 1]).then_inc(s_xn, 1)
                act.wait_ge(s_xn, (BLK - BLK_POOL) * (b + 1))
                act.wait_ge(s_xnp, BLK_POOL * (b + 1))
                if b >= 2:
                    act.wait_ge(s_tab[b % 2], 64 * (b // 2))
                o = (b % 2) * BLK
                copy(gring[0:TN, o:o + BLK, 0:D], x_all[:, b * BLK:(b + 1) * BLK, :]).then_inc(s_hi16, 1)
            act.wait_ge(s_wprep, 2)
            copy(wkv_hi[:, :, :], wstage[:, :, :]).then_inc(s_wsplit, 1)
            act.wait_ge(s_w2, 16)
            copy(w2_hi[:, :, :], w2_sb).then_inc(s_ca, 1)
            act.wait_ge(s_const, 10)
            nc.scalar.activation(tab_in[:, 1:2], tab_in[:, 0:1], ACT.Sqrt)
            act.wait_ge(s_pz, 2)

            def flush(it, u):
                act.wait_ge(s_seg[1], fin(it, 1))
                act.wait_ge(s_tp, fin(it, 2))
                act.wait_ge(s_pj, fin(it, 2))
                copy(fl[:, :], ps_seg[1 - u][:, D:2 * D]).then_inc(s_fl, 1)
                copy(fl_t[:, 0:KC, :], ps_seg[1 - u][:, 0:D].rearrange("p (c n) -> p c n", c=KC)).then_inc(s_flx, 1)

            def flush_t(it):
                act.wait_ge(s_tp, fin(it, 1))
                copy(fl_t[:, KC:, :], ps_t[:, 0:D].rearrange("p (c n) -> p c n", c=KC)).then_inc(s_flt, 1)

            def epilogue(it):
                flush(it, 0)
                flush_t(it)

            def prepare(it, u, pair, h):
                act.wait_ge(s_e[u][h], 16 * (pair + 1))
                act.wait_ge(s_edge[h], fin(it, 1))
                copy(e_hi[:, h * HT:(h + 1) * HT, :], e32[:, h * HT:(h + 1) * HT, :]).then_inc(s_ehi[h], 1)

            def prepare16(it, h):
                act.wait_ge(s_hot[h], fin(it))
                act.wait_ge(s_seg[h], fin(it, 1))
                act.wait_ge(s_edge[1], fin(it, 1))
                copy(s16[:, h * HT:(h + 1) * HT, :], s32[:, h * HT:(h + 1) * HT, :].bitcast(F32)).then_inc(s_hot16[h], 1)

            def first_half(it, pair):
                prepare(it, 0, pair, 0)
                prepare16(it, 0)

            def body(it, u, pair, kv=None, mix=None, g=None, ahead=True, put=None, lap=0, i=None, fold=None):
                if kv is not None:
                    act.wait_ge(s_xl[u], 16 * (pair + 1))
                    act.wait_ge(s_xt, fin(kv, 1))
                    nc.scalar.activation(xnc[:, 0, :], xch[:, u, 0, :], ACT.Identity, bias=nmr1[:, ds(kv, 1)],
                                         scale=r1[:, ds(kv, 1)]).then_inc(s_xst, 1)
                if mix is not None:
                    act.wait_ge(s_xl[u], (pair + (1 - G_MIX // 2 + NT // 2)) * 16)
                    act.wait_ge(s_b1, mix * 2 + 1)
                    for j in range(2):
                        nc.scalar.activation(xnc[:, j, :], xch[:, u, j, :], ACT.Identity, bias=nmr1[:, ds(mix * 2 + j, 1)],
                                             scale=r1[:, ds(mix * 2 + j, 1)]).then_inc(s_xst, 1)
                flush(it, u)
                if mix is not None:
                    act.wait_ge(s_xt, fin(mix + NT))
                    act.wait_ge(s_hp, fin(mix, 1))
                    copy(xt_hi[:, :, 0:CN], ps_xt[:, 0:KC * CN].rearrange("p (c n) -> p c n", c=KC)).then_inc(s_xhi, 1)
                prepare(it, u, pair, 1)
                prepare16(it, 1)
                if kv is not None:
                    act.wait_ge(s_xt, fin(kv))
                    act.wait_ge(s_kvp, fin(kv, 1))
                    copy(xt_hi[:, :, 0:TN], ps_xt[:, 0:KC * TN].rearrange("p (c n) -> p c n", c=KC)).then_inc(s_xhi, 1)
                flush_t(it)
                if mix is not None:
                    put = mix - 1
                if put is not None:
                    act.wait_ge(s_bs, fin(put))
                    act.dma_start(base_d[ds(put * CN + CN, CN), :].rearrange("(t p) d -> p t d", p=TN),
                                  xch[:, 1 - u, :, :]).then_inc(s_bd[1 - u], 16)
                if mix is not None:
                    act.wait_ge(s_hp, fin(mix))
                    act.wait_ge(s_hlo, fin(mix, 1))
                    for f in range(KC):
                        gelu = nc.scalar.activation(hm[:, f, 0:CN], ps_kv[:, f * CW:f * CW + CN], ACT.Gelu, bias=bm[:, f:f + 1])
                    gelu.then_inc(s_hg, 1)
                    act.wait_ge(s_hg, fin(mix))
                    act.wait_ge(s_mp, fin(mix, 1))
                    copy(hm_hi[:, :, 0:CN], hm[:, :, 0:CN]).then_inc(s_hhi, 1)
                if ahead:
                    prepare(it + 1, 1 - u, pair + u, 0)
                if kv is not None:
                    act.wait_ge(s_xc, fin(kv))
                    act.wait_ge(s_kva, fin(kv))
                    nc.scalar.activation(kvn, xc, ACT.Square).then_inc(s_sq, 1)
                    act.wait_ge(s_ve, fin(kv))
                    nc.scalar.activation(lnst[:, 2, :], lnst[:, 1, :], ACT.Sqrt).then_inc(s_sd, 1)
                if ahead:
                    prepare16(it + 1, 0)

            def between(step):
                if step == 2:
                    nc.scalar.activation(tab_in[:, 2:3], tab_in[:, 0:1], ACT.Gelu)
                    act.wait_ge(s_c, 3)
                    copy(m_hi[:, :, :], p_sb[:, :, :]).then_inc(s_ca, 1)

            first_half(0, 0)
            schedule(act, body, between)
            general(act, body, lambda k: first_half(k * NG, k * (NG // 2)), epilogue)

            act.wait_ge(s_sums, 1)
            act.sem_inc(s_fz[0], 2)
            act.sem_inc(s_fz[1], 2)
            act.sem_inc(s_kept, 2)
            act.wait_ge(s_nd, 2)
            nc.scalar.activation(degs[:, 1, :], degs[:, 0, :], ACT.Sqrt).then_inc(s_na, 1)

            def stage(c, u, i):
                act.wait_ge(s_ft[u], i + 1)
                copy(y_st[:, u, :, :], acc_y[:, :, ds(c * CN, CN)]).then_inc(s_y, 1)

            def scaled(c, u, i):
                act.wait_ge(s_ft[u], i + 2)
                act.wait_ge(s_kept, c + 1)
                for j in range(2):
                    nc.scalar.activation(y_n[:, u, j, :], bank[u][0:TN, j * D:(j + 1) * D], ACT.Identity,
                                         scale=norm[:, ds(c * 2 + j, 1)]).then_inc(s_fz[u], 1)

            def deviation(c, u):
                act.wait_ge(s_fv, c * 2 + 1)
                nc.scalar.activation(sdn[:, u, :], ven[:, u, :], ACT.Sqrt).then_inc(s_sdn, 1)

            def step(c, u, i):
                act.wait_ge(s_fx[u], i + 2)
                copy(x2[:, ds(c * 2, 2), :], y_n[:, u, :, :]).then_inc(s_kept, 1)
                deviation(c, u)
                if not (isinstance(c, int) and c + 2 >= NC):
                    scaled(c + 2, u, i + 1)
                if not (isinstance(c, int) and c + 4 >= NC):
                    stage(c + 4, u, i + 2)

            stage(0, 0, 0)
            stage(1, 1, 0)
            act.wait_ge(s_nd, 4)
            scaled(0, 0, 0)
            scaled(1, 1, 0)
            stage(2, 0, 1)
            stage(3, 1, 1)
            node_chunks(act, step)

            def rows(c, u, i):
                wait_past(act, s_xlb[u], i)
                wait_past(act, s_xtp[u], i)
                for j in range(2):
                    nc.scalar.activation(xl[:, u, j, :], x2[:, ds(c * 2 + j, 1), :], ACT.Identity, bias=nmr2[:, ds(c * 2 + j, 1)],
                                         scale=r2[:, ds(c * 2 + j, 1)]).then_inc(s_xl2[u], 1)

            def rows_hi(c, u, i):
                act.wait_ge(s_xtp[u], i + 1)
                copy(xf_hi[:, :, 0:CN], ps_xt[:, 0:KC * CN].rearrange("p (c n) -> p c n", c=KC)).then_inc(s_xfh, 1)

            def hidden(c, u, i):
                for q in range(FC // 2):
                    act.wait_ge(s_g1, c * (FC // 2) + (q + 1))
                    if not (isinstance(c, int) and c == 0):
                        act.wait_ge(s_hl, c * (FC // 2) + (q + 1 - FC // 2))
                    for f in range(2 * q, 2 * q + 2):
                        nc.scalar.activation(h32[:, f, :], bank[q][:, (f % 2) * CW:(f % 2 + 1) * CW], ACT.Gelu,
                                             bias=fb1c[:, f:f + 1]).then_inc(s_ge, 1)
                    act.wait_ge(s_ge, c * FC + (2 * q + 2))
                    wait_past(act, s_g2[u], i)
                    copy(h_hi[:, u, 2 * q:2 * q + 2, :], h32[:, 2 * q:2 * q + 2, :]).then_inc(s_hh, 1)

            def normed(c, u, i):
                act.wait_ge(s_bnx, c + 1)
                wait_past(act, s_out[u], i * 16)
                for j in range(2):
                    nc.scalar.activation(res[:, u, j, :], o_sb[:, u, j, :], ACT.Identity, bias=bnx[:, u, j:j + 1],
                                         scale=rx[:, u, j:j + 1]).then_inc(s_rn[u], 1)

            def step(c, u, i):
                fixed = isinstance(c, int)
                if not (fixed and c + 2 >= NC):
                    rows(c + 2, u, i + 1)
                if not (fixed and c + 1 >= NC):
                    hidden(c + 1, 1 - u, i + u)
                if not (fixed and c + 2 >= NC):
                    rows_hi(c + 2, u, i + 1)
                if not (fixed and c == 0):
                    normed(c - 1, 1 - u, i + (u - 1))

            act.wait_ge(s_r2, 4 + 2 * 2)
            act.wait_ge(s_kept, 4)
            rows(0, 0, 0)
            rows(1, 1, 0)
            rows_hi(0, 0, 0)
            act.wait_ge(s_rd, 5)
            nc.scalar.activation(rt[0:1, 2, :], rt[0:1, 1, :], ACT.Exp, bias=rs[0:1, 1:2]).then_inc(s_ra, 1)
            act.wait_ge(s_rd, 16)
            nc.scalar.activation(rt[0:1, 9, :], rt[0:1, 8, :], ACT.Exp, bias=rs[0:1, 5:6]).then_inc(s_ra, 1)
            act.wait_ge(s_rd, 21)
            nc.scalar.activation(rt[0:1, 12, 0:2], rt[0:1, 11, 0:2], ACT.Exp, bias=rs[0:1, 8:9]).then_inc(s_ra, 1)

            act.wait_ge(s_ra, 3)
            nc.scalar.activation(rt[0:1, 14, 0:1], rt[0:1, 12, 0:1], ACT.Gelu)
            for j in range(2):
                act.wait_ge(s_fw1[j], 16)
                copy(fw1_hi[:, :, j * F:(j + 1) * F], fw1_st[:, j, :, :]).then_inc(s_w1h, 1)
            for j in range(2):
                act.wait_ge(s_w2s, j + 1)
                copy(fw2_hi[:, j * (FC // 2):(j + 1) * (FC // 2), :], fw2_st[:, j, :, :]).then_inc(s_w2h, 1)
            act.wait_ge(s_fb, 16 * 6)

            hidden(0, 0, 0)
            rows_hi(1, 1, 0)
            chunks(act, step)
            normed(NC - 1, (NC - 1) % 2, NC // 2)

        @block.tensor
        def _(pe):
            pe.sem_inc(s_seg[0], 2)
            pe.sem_inc(s_seg[1], 2)
            pe.sem_inc(s_edge[0], 2)
            pe.sem_inc(s_edge[1], 2)
            pe.sem_inc(s_tp, 1)
            pe.sem_inc(s_pj, 1)
            for s in (s_xt, s_kvp, s_kva, s_hp, s_mp):
                pe.sem_inc(s, 2)
            pe.wait_ge(s_id, 2)
            pe.wait_ge(s_const, 10)
            pe.wait_ge(s_d, 2)
            pe.transpose(ps_t[0:NG, 0:P], gmin[:, :], ident[:, :]).then_inc(s_dp, 1)
            pe.wait_ge(s_d, 4)
            pe.matmul(ps_y[:, 0:NG], lhsT=bcol_w[:, :], rhs=ident[0:NG, 0:NG], start=True, stop=True).then_inc(s_dp, 1)
            pe.wait_ge(s_d, 8)
            pe.transpose(ps_t[0:1, 0:P], okc[:, 0:1], ident[:, :]).then_inc(s_dp, 1)
            pe.wait_ge(s_d, 10)
            pe.matmul(ps_xt[:, 0:1], lhsT=ones[0:1, :], rhs=okc[0:1, 2:3], start=True, stop=True).then_inc(s_dp, 1)
            pe.matmul(ps_acc[:, 0:KC * P], lhsT=xt_hi[:, 0, 0:P], rhs=xt_lo[:, 0, :], start=True, stop=True, skip_group_check=True)
            pe.wait_ge(s_par, 16 * 11)
            pe.wait_ge(s_wsplit, 2)
            pe.wait_ge(s_d, 12)

            def products(hi, lo):
                return ((hi[0], hi[1]), (hi[0], lo[1]), (lo[0], hi[1]))

            def transposes(it):
                pe.wait_ge(s_fl, fin(it, 1))
                pe.wait_ge(s_flt, fin(it, 2))
                for c in range(KC):
                    mm = pe.transpose(ps_t[:, c * W:(c + 1) * W], fl[:, c * P:(c + 1) * P], ident[:, :])
                mm.then_inc(s_tp, 1)

            def project(it):
                pe.wait_ge(s_flx, fin(it, 1))
                pe.wait_ge(s_flt, fin(it, 1))
                pe.wait_ge(s_acc, fin(it, 2))
                for o in range(KC):
                    for c in range(4):
                        mm = pe.matmul(ps_y[:, o * W:(o + 1) * W], lhsT=wg[:, c, o * P:(o + 1) * P], rhs=fl_t[:, c, :],
                                       start=c == 0, stop=c == 3)
                mm.then_inc(s_pj, 1)

            def epilogue(it):
                transposes(it)
                project(it)

            def edge_part(it, u, h, tiles=ALL):
                pe.wait_ge(s_hot[h], fin(it))
                pe.wait_ge(s_ehi[h], fin(it))
                if h == 1:
                    pe.wait_ge(s_hot16[0], fin(it))
                    pe.wait_ge(s_hot16[1], fin(it))
                    pe.wait_ge(s_dacc, fin(it, 1))
                    for k in tiles:
                        pe.matmul(ps_deg[0:1, 0:W], lhsT=ones16[:, :], rhs=s16[:, k, :], start=k == 0, stop=k == tiles[-1])
                if h == 0:
                    pe.wait_ge(s_flx, fin(it, 2))
                mine = [k for k in slots[h] if k in tiles]
                for k in mine:
                    pe.matmul(ps_seg[u][:, D:2 * D], lhsT=s32[:, k, :], rhs=e_hi[:, k, :], start=k == 0, stop=False, skip_group_check=True)
                pe.wait_ge(s_elo[h], fin(it))
                for k in mine:
                    mm = pe.matmul(ps_seg[u][:, D:2 * D], lhsT=s32[:, k, :], rhs=e_lo[:, k, :], start=False, stop=k == tiles[-1], skip_group_check=True)
                mm.then_inc(s_edge[h], 1)

            def x_part(it, u, pair, h, lap, i, tiles=ALL):
                mine = [k for k in slots[h] if k in tiles]
                pe.wait_ge(s_hot16[h], fin(it))
                done = (pair if i is None else i) * (16 * HT) + lap * (NG // 2 * 16 * HT - u * 16 * (HT - 1))
                pe.wait_ge(s_gat[u][h], done + 16 * len(mine))
                for k in mine:
                    for j in range(2):
                        for c in range(KC):
                            mm = pe.matmul(ps_seg[u][:, c * W:(c + 1) * W], lhsT=gring[:, u * GT + k, j * D + c * P:j * D + (c + 1) * P],
                                           rhs=s16[:, k, :], start=False, stop=k == tiles[-1] and j == 1, skip_group_check=True)
                mm.then_inc(s_seg[h], 1)

            def fold_weights(step):
                if step == 1:
                    pe.wait_ge(s_c, 1)
                    for h in range(KC):
                        mm = pe.matmul(ps_kv[:, h * D:(h + 1) * D], lhsT=kv_t[:, h, :], rhs=w1_sb[:, h, :], start=True, stop=True)
                    mm.then_inc(s_cp, 1)
                if step == 2:
                    pe.wait_ge(s_c, 2)
                    pe.wait_ge(s_xlo, NT + 2)
                    for o in range(KC):
                        for c in range(KC):
                            pe.matmul(ps_xt[:, o * D:(o + 1) * D], lhsT=wq_sb[:, c, o * P:(o + 1) * P], rhs=p_sb[:, c, :], start=c == 0, stop=c == KC - 1)
                    for f in range(KC):
                        for c in range(KC):
                            mm = pe.matmul(ps_acc[:, f:f + 1], lhsT=p_sb[:, c, f * P:(f + 1) * P], rhs=bq[:, c:c + 1], start=c == 0, stop=c == KC - 1)
                    mm.then_inc(s_cp, 1)

            def accumulate():
                for h in range(KC):
                    mm = pe.matmul(ps_acc[:, h * P:(h + 1) * P], lhsT=kvn[:, D + h * P:D + (h + 1) * P], rhs=kvn[:, h * P:(h + 1) * P],
                                   start=False, stop=True, skip_group_check=True)
                mm.then_inc(s_kva, 1)

            def body(it, u, pair, kv=None, mix=None, g=None, ahead=True, put=None, lap=0, i=None, fold=None):
                edge_part(it, u, 0)
                if kv is not None:
                    pe.wait_ge(s_kvn, fin(kv, 1))
                    accumulate()
                    pe.wait_ge(s_xst, fin(kv))
                    pe.wait_ge(s_xlo, fin(kv, 1))
                    for c in range(KC):
                        mm = pe.transpose(ps_xt[:, c * TN:(c + 1) * TN], xnc[:, 0, c * P:(c + 1) * P], ident[0:TN, 0:TN])
                    mm.then_inc(s_xt, 1)
                if mix is not None:
                    pe.wait_ge(s_xst, mix * 2 + (NT + 4))
                    pe.wait_ge(s_xlo, fin(mix + NT, 1))
                    for j in range(2):
                        for c in range(KC):
                            mm = pe.transpose(ps_xt[:, c * CN + j * TN:c * CN + (j + 1) * TN], xnc[:, j, c * P:(c + 1) * P], ident[0:TN, 0:TN])
                    mm.then_inc(s_xt, 1)
                x_part(it, u, pair, 0, lap, i)
                transposes(it)
                if kv is not None:
                    pe.wait_ge(s_xhi, fin(kv))
                    pe.wait_ge(s_xlo, fin(kv))
                    pe.wait_ge(s_xc, fin(kv, 1))
                    ops = [(a[:, c, 0:TN], b[:, c, :]) for c in range(KC) for a, b in products((xt_hi, wkv_hi), (xt_lo, wkv_lo))]
                    for n, (a, b) in enumerate(ops):
                        mm = pe.matmul(ps_kv[0:TN, :], lhsT=a, rhs=b, start=n == 0, stop=n == len(ops) - 1)
                    mm.then_inc(s_kvp, 1)
                if mix is not None:
                    pe.wait_ge(s_xhi, fin(mix + NT))
                    pe.wait_ge(s_xlo, fin(mix + NT))
                    pe.wait_ge(s_hg, fin(mix, 1))
                    for f in range(KC):
                        ops = [(a[:, c, f * P:(f + 1) * P], b[:, c, :]) for c in range(KC) for a, b in products((m_hi, xt_hi), (m_lo, xt_lo))]
                        for n, (a, b) in enumerate(ops):
                            mm = pe.matmul(ps_kv[:, f * CW:(f + 1) * CW], lhsT=a, rhs=b, start=n == 0, stop=n == len(ops) - 1)
                    mm.then_inc(s_hp, 1)
                project(it)
                if fold is not None:
                    fold_weights(fold)
                edge_part(it, u, 1)
                if mix is not None:
                    pe.wait_ge(s_hhi, fin(mix))
                    pe.wait_ge(s_hlo, fin(mix))
                    pe.wait_ge(s_bs, fin(mix, 1))
                    for j in range(2):
                        ops = [(a[:, f, j * TN:(j + 1) * TN], b[:, f, :]) for f in range(KC) for a, b in products((hm_hi, w2_hi), (hm_lo, w2_lo))]
                        for n, (a, b) in enumerate(ops):
                            mm = pe.matmul(ps_acc[0:TN, j * D:(j + 1) * D], lhsT=a, rhs=b, start=n == 0, stop=n == len(ops) - 1)
                    mm.then_inc(s_mp, 1)
                x_part(it, u, pair, 1, lap, i)

            def last(it, u, pair, g=None, ahead=True, lap=0, i=None):
                if u == 0:
                    body(it, u, pair, lap=lap, i=i)
                    return
                edge_part(it, u, 0, SHORT)
                x_part(it, u, pair, 0, lap, i, SHORT)
                transposes(it)
                project(it)
                edge_part(it, u, 1, SHORT)
                x_part(it, u, pair, 1, lap, i, SHORT)

            def between(step):
                if step == 0:
                    pe.wait_ge(s_kvn, NT + 2)
                    accumulate()
                if step == 2:
                    pe.wait_ge(s_c, 6)
                    pe.wait_ge(s_ca, 2)

            schedule(pe, body, between, last)
            general(pe, body, epilogue=epilogue, last=last)

            pe.wait_ge(s_sums, 1)
            pe.wait_ge(s_dg, 32)
            pe.transpose(ps_t[0:TN, 0:NT], deg_t[:, :], ident[0:NT, 0:NT]).then_inc(s_np, 1)
            pe.sem_inc(s_ft[0], 1)
            pe.sem_inc(s_ft[1], 1)
            pe.sem_inc(s_mean, 2)
            ps_mean = ps_kv
            pe.wait_ge(s_nd, 1)
            for c in range(KC):
                pe.matmul(ps_mean[0:1, c * P:(c + 1) * P], lhsT=zcol[:, :], rhs=ones[:, :], start=c == 0, stop=True, skip_group_check=True)

            def rows(c, u, i):
                pe.wait_ge(s_y, c + 1)
                pe.wait_ge(s_fz[u], i * 2 + 2)
                for j in range(2):
                    for o in range(KC):
                        mm = pe.transpose(bank[u][0:TN, j * D + o * P:j * D + (o + 1) * P], y_st[:, u, o, j * TN:(j + 1) * TN], ident[:, :])
                mm.then_inc(s_ft[u], 1)

            def mean(c, u):
                pe.wait_ge(s_rst, c + 1)
                pe.wait_ge(s_kept, c + 3)
                for j in range(2):
                    mm = pe.matmul(ps_mean[0:1, 0:D], lhsT=rst[:, u, j:j + 1], rhs=x2[:, ds(c * 2 + j, 1), :], start=False, stop=True, skip_group_check=True)
                mm.then_inc(s_mean, 1)

            def step(c, u, i):
                mean(c, u)
                if not (isinstance(c, int) and c + 4 >= NC):
                    rows(c + 4, u, i + 2)

            for c in range(4):
                rows(c, c % 2, c // 2)
            node_chunks(pe, step)
            ps_o = [ps_kv, ps_acc]

            def turn(c, u, i):
                pe.wait_ge(s_xl2[u], i * 2 + 2)
                wait_past(pe, s_xfl, c)
                for j in range(2):
                    for o in range(KC):
                        mm = pe.transpose(ps_xt[:, o * CN + j * TN:o * CN + (j + 1) * TN], xl[:, u, j, o * P:(o + 1) * P], ident[0:TN, 0:TN])
                mm.then_inc(s_xtp[u], 1)

            def first(c, u, i):
                pe.wait_ge(s_xfh, c + 1)
                pe.wait_ge(s_xfl, c + 1)
                for f in range(FC):
                    q = f // 2
                    if f % 2 == 0 and not (isinstance(c, int) and c == 0):
                        pe.wait_ge(s_ge, c * FC + (2 * q + 2 - FC))
                    ops = [(a[:, k, f * P:(f + 1) * P], b[:, k, :]) for k in range(KC) for a, b in products((fw1_hi, xf_hi), (fw1_lo, xf_lo))]
                    for n, (a, b) in enumerate(ops):
                        mm = pe.matmul(bank[q][:, (f % 2) * CW:(f % 2 + 1) * CW], lhsT=a, rhs=b, start=n == 0, stop=n == len(ops) - 1)
                    if f % 2:
                        mm.then_inc(s_g1, 1)

            def second(c, u, i):
                pe.wait_ge(s_hh, c * (FC // 2) + FC // 2)
                pe.wait_ge(s_hl, c * (FC // 2) + FC // 2)
                wait_past(pe, s_od[u], i)
                for j in range(2):
                    ops = [(a[:, u, f, j * TN:(j + 1) * TN], b[:, f, :]) for f in range(FC) for a, b in products((h_hi, fw2_hi), (h_lo, fw2_lo))]
                    for n, (a, b) in enumerate(ops):
                        mm = pe.matmul(ps_o[u][0:TN, j * D:(j + 1) * D], lhsT=a, rhs=b, start=n == 0, stop=n == len(ops) - 1)
                mm.then_inc(s_g2[u], 1)

            def step(c, u, i):
                fixed = isinstance(c, int)
                if not (fixed and c + 1 >= NC):
                    first(c + 1, 1 - u, i + u)
                if not (fixed and c + 2 >= NC):
                    turn(c + 2, u, i + 1)
                second(c, u, i)

            turn(0, 0, 0)
            pe.wait_ge(s_rd, 1)
            pe.matmul(ps_t[0:1, 0:1], lhsT=nsum[:, :], rhs=ones[0:TN, 0:1], start=True, stop=True).then_inc(s_rp, 1)
            pe.wait_ge(s_rd, 2 + 1)
            for c in range(KC):
                mm = pe.matmul(ps_y[:, c:c + 1], lhsT=mrow[0:1, c * P:(c + 1) * P], rhs=ones[0:1, 0:1], start=True, stop=True)
            mm.then_inc(s_rp, 1)
            pe.wait_ge(s_rm, 1)
            pe.wait_ge(s_rw, 32)
            for c in range(KC):
                mm = pe.matmul(ps_t[0:1, 0:EX], lhsT=mean_c[:, c:c + 1], rhs=wr_sb[:, c, :], start=c == 0, stop=c == KC - 1)
            mm.then_inc(s_rp, 1)
            pe.wait_ge(s_top, 2)
            pe.matmul(ps_y[:, 0:2], lhsT=ones[0:1, :], rhs=rt[0:1, 13, 0:2], start=True, stop=True).then_inc(s_bp, 1)
            pe.wait_ge(s_w1l, 4)
            first(0, 0, 0)
            turn(1, 1, 0)
            pe.wait_ge(s_w2s, 4)
            for j in range(2):
                mm = pe.matmul(ps_acc[0:TN, 0:D], lhsT=ones[0:1, 0:TN], rhs=fb2r[0:1, j, :], start=j == 0, stop=j == 1)
            mm.then_inc(s_bp, 1)

            pe.wait_ge(s_w2l, 2)
            pe.wait_ge(s_b2w, 1)
            chunks(pe, step)

        @block.vector
        def _(v):
            for s in (s_idx, s_hot[0], s_hot[1], s_elo[0], s_elo[1], s_xlo, s_xc, s_ve, s_kvn, s_hlo, s_b1, s_bs):
                v.sem_inc(s, 2)
            v.sem_inc(s_acc, 1)
            v.sem_inc(s_dacc, 1)
            v.memset(ps_seg[1][:, :], 0.0).then_inc(s_pz, 1)
            v.memset(ps_deg[0:1, 0:W], 0.0).then_inc(s_pz, 1)
            v.memset(brow[:, :], 0).then_inc(s_br, 1)

            def stats(b):
                v.wait_ge(s_x[b], 32)
                if b:
                    v.wait_ge(s_mv, BLK * b)
                for j in range(BLK):
                    v.bn_stats(st6[:, j, :], x_all[:, b * BLK + j, :]).then_inc(s_st, 1)
                if b:
                    v.wait_ge(s_r1, b)
                for j in range(BLK):
                    v.wait_ge(s_st, b * BLK + j + 1)
                    v.bn_aggr(mvs[:, j, :], st6[:, j, :]).then_inc(s_mv, 1)

            def low(b):
                o = (b % 2) * BLK
                v.wait_ge(s_hi16, b + 1)
                v.tensor_tensor(gring[0:TN, o:o + BLK, D:2 * D], x_all[:, b * BLK:(b + 1) * BLK, :], gring[0:TN, o:o + BLK, 0:D],
                                ALU.subtract).then_inc(s_lo16, 1)

            v.wait_ge(s_dst, 16)
            v.tensor_copy(rel[:, :], dst_i).then_inc(s_d, 1)
            v.wait_ge(s_d, 1)
            v.tensor_reduce(gmin[:, :], rel_g, AX, ALU.min).then_inc(s_d, 1)
            v.wait_ge(s_dp, 1)
            v.tensor_reduce(bcol[:, :], ps_t[0:NG, 0:P], AX, ALU.min).then_inc(s_d, 1)
            v.wait_ge(s_d, 3)
            v.tensor_scalar(bcol_w[:, :], ones[0:NG, :], bcol[:, 0:1], None, ALU.mult).then_inc(s_d, 1)
            v.wait_ge(s_dp, 2)
            v.tensor_copy(bwide[:, :], ps_y[:, 0:NG]).then_inc(s_d, 1)
            def take(g, u):
                v.tensor_copy(idx[:, u * GT:(u + 1) * GT], src_sb[:, ds(g * GT, GT)]).then_inc(s_idx, 1)

            stats(0)
            stats(1)
            v.wait_ge(s_d, 5)
            v.tensor_tensor(rel_g, rel_g, wide(bwide[:, :], NG, GT), ALU.subtract).then_inc(s_d, 1)
            v.wait_ge(s_d, 6)
            v.scalar_tensor_tensor(rel_tmp, rel[:, :], MASKED / 10, rel[:, :], ALU.is_lt, ALU.mult).then_inc(s_d, 1)
            v.wait_ge(s_d, 7)
            v.tensor_reduce(okc[:, 0:1], rel_tmp, AX, ALU.max).then_inc(s_d, 1)
            stats(2)
            low(0)
            stats(3)
            low(1)
            stats(4)
            low(2)
            v.wait_ge(s_src, 16)
            take(0, 0)
            v.wait_ge(s_dp, 3)
            v.tensor_reduce(okc[0:1, 1:2], ps_t[0:1, 0:P], AX, ALU.max).then_inc(s_d, 1)
            v.wait_ge(s_d, 9)
            v.tensor_scalar(okc[0:1, 2:3], okc[0:1, 1:2], float(W), None, ALU.is_lt).then_inc(s_d, 1)
            v.wait_ge(s_d, 10)
            v.tensor_copy(ok_i[:, :], okc[0:1, 2:3]).then_inc(s_d, 1)
            v.wait_ge(s_dp, 4)
            v.tensor_scalar(okc[:, 3:4], ps_xt[:, 0:1], -1.0, 1.0, ALU.mult, ALU.add).then_inc(s_d, 1)
            v.wait_ge(s_d, 12)
            v.tensor_scalar(gmin[:, :], bwide[:, :], okc[:, 3:4], None, ALU.mult).then_inc(s_d, 1)
            v.wait_ge(s_d, 13)
            v.tensor_tensor(rel_g, rel_g, wide(gmin[:, :], NG, GT), ALU.add).then_inc(s_d, 1)
            v.tensor_tensor(bwide[:, :], bwide[:, :], gmin[:, :], ALU.subtract).then_inc(s_d, 1)
            v.wait_ge(s_d, 15)
            v.wait_ge(s_br, 1)
            v.tensor_copy(brow[0:1, 1:NG + 1], bwide[0:1, :]).then_inc(s_rel, 1)
            low(3)
            low(4)
            v.wait_ge(s_iota, 1)
            v.tensor_copy(iota[:, :], iota_i[:, :]).then_inc(s_iota, 1)
            v.wait_ge(s_wkv, 16 * 6)
            wv = wstage[:, :, :].rearrange("p c (g e) -> p (c g) e", e=HC)
            v.tensor_reduce(wmean[:, :], wv, AX, ALU.add).then_inc(s_wprep, 1)
            v.wait_ge(s_wprep, 1)
            v.scalar_tensor_tensor(wv, wide(wmean[:, :], KC * GR, HC), -1.0 / HC, wv, ALU.mult, ALU.add).then_inc(s_wprep, 1)
            bv = bkv[:, :].rearrange("p (g e) -> p g e", e=HC)
            v.tensor_reduce(lnst[:, 0, :], bv, AX, ALU.add).then_inc(s_wprep, 1)
            v.wait_ge(s_wprep, 3)
            v.scalar_tensor_tensor(bv, wide(lnst[:, 0, :], GR, HC), -1.0 / HC, bv, ALU.mult, ALU.add).then_inc(s_wprep, 1)
            v.wait_ge(s_par, 16 * 11)
            v.tensor_tensor(brows[:, :], brows[:, :], hrows[:, :], ALU.add).then_inc(s_br, 1)
            v.wait_ge(s_wsplit, 1)
            v.tensor_tensor(wkv_lo[:, :, :], wstage[:, :, :], wkv_hi[:, :, :].bitcast(F32), ALU.subtract).then_inc(s_wsplit, 1)

            v.wait_ge(s_rel, 1)
            v.wait_ge(s_iota, 2)
            v.wait_ge(s_wprep, 4)
            v.wait_ge(s_br, 2)
            v.wait_ge(s_pz, 2)
            v.wait_ge(s_zero, 1 + NT // BLK)

            def one_hot(it, g, h):
                a, z = h * HT, (h + 1) * HT
                v.wait_ge(s_edge[h], fin(it, 1))
                v.wait_ge(s_hot16[h], fin(it, 1))
                v.tensor_tensor(s32[:, a:z, :], iota[:, :].unsqueeze(1).broadcast_to([P, HT, W]),
                                rel[:, ds(g * GT + a, HT)].unsqueeze(2).broadcast_to([P, HT, W]), ALU.is_equal).then_inc(s_hot[h], 1)

            def low_edges(it, h):
                a, z = h * HT, (h + 1) * HT
                v.wait_ge(s_ehi[h], fin(it))
                v.tensor_tensor(e_lo[:, a:z, :], e32[:, a:z, :], e_hi[:, a:z, :].bitcast(F32), ALU.subtract).then_inc(s_elo[h], 1)

            def degrees(it, g):
                b = v.value_load(brow[0:1, ds(g, 1)], min_val=0, max_val=NPAD - W)
                v.wait_ge(s_seg[1], fin(it, 1))
                v.wait_ge(s_dacc, fin(it, 2))
                v.tensor_tensor(deg_row[0:1, ds(b, W)], deg_row[0:1, ds(b, W)], ps_deg[0:1, 0:W], ALU.add).then_inc(s_dacc, 1)
                return b

            def flush(it, b):
                v.wait_ge(s_pj, fin(it, 1))
                v.wait_ge(s_acc, fin(it, 2))
                v.tensor_tensor(acc_y[:, :, ds(b, W)], acc_y[:, :, ds(b, W)], ps_y[:, 0:KC * W].rearrange("p (c n) -> p c n", c=KC),
                                ALU.add).then_inc(s_acc, 1)

            def body(it, u, pair, kv=None, mix=None, g=None, ahead=True, put=None, lap=0, i=None, fold=None):
                g = it if g is None else g
                one_hot(it, g, 1)
                if mix is not None:
                    v.wait_ge(s_xhi, fin(mix + NT))
                    v.tensor_tensor(xt_lo[:, :, 0:CN], ps_xt[:, 0:KC * CN].rearrange("p (c n) -> p c n", c=KC),
                                    xt_hi[:, :, 0:CN].bitcast(F32), ALU.subtract).then_inc(s_xlo, 1)
                if mix is None:
                    low_edges(it, 1)
                b = degrees(it, g)
                if ahead:
                    take(g + 1, 1 - u)
                if mix is not None:
                    low_edges(it, 1)
                if kv is not None:
                    v.wait_ge(s_xhi, fin(kv))
                    v.tensor_tensor(xt_lo[:, :, 0:TN], ps_xt[:, 0:KC * TN].rearrange("p (c n) -> p c n", c=KC),
                                    xt_hi[:, :, 0:TN].bitcast(F32), ALU.subtract).then_inc(s_xlo, 1)
                if mix is not None:
                    v.wait_ge(s_xst, mix * 2 + (NT + 4))
                    v.tensor_tensor(xch[:, u, :, :], xnc[:, :, :], xch[:, u, :, :], ALU.add).then_inc(s_b1, 1)
                    v.wait_ge(s_b1, mix * 2 + 3)
                    v.tensor_tensor(xch[:, u, :, :], xch[:, u, :, :], brows[:, :].unsqueeze(1).broadcast_to([TN, 2, D]), ALU.add).then_inc(s_b1, 1)
                if ahead:
                    one_hot(it + 1, g + 1, 0)
                if kv is not None:
                    v.wait_ge(s_kvp, fin(kv))
                    v.wait_ge(s_sq, fin(kv, 1))
                    v.tensor_tensor(xc, ps_kv[0:TN, :], bkv[:, :], ALU.add).then_inc(s_xc, 1)
                if mix is not None:
                    v.wait_ge(s_hhi, fin(mix))
                    v.tensor_tensor(hm_lo[:, :, 0:CN], hm[:, :, 0:CN], hm_hi[:, :, 0:CN].bitcast(F32), ALU.subtract).then_inc(s_hlo, 1)
                if ahead:
                    low_edges(it + 1, 0)
                flush(it, b)
                if kv is not None:
                    kvg = kvn.rearrange("p (g e) -> p g e", e=HC)
                    kvh = kvn.rearrange("p (s h e) -> p s h e", s=2, e=HC)
                    v.wait_ge(s_sq, fin(kv))
                    v.tensor_reduce(lnst[:, 0, :], kvg, AX, ALU.add).then_inc(s_kd, 1)
                    v.wait_ge(s_kd, kv * 4 + 1)
                    v.tensor_scalar(lnst[:, 1, :], lnst[:, 0, :], 1.0 / HC, EPS, ALU.mult, ALU.add).then_inc(s_ve, 1)
                    v.wait_ge(s_sd, fin(kv))
                    v.reciprocal(lnst[:, 3, :], lnst[:, 2, :]).then_inc(s_kd, 1)
                    v.wait_ge(s_kd, kv * 4 + 2)
                    v.tensor_tensor(kvg, xc.rearrange("p (g e) -> p g e", e=HC), wide(lnst[:, 3, :], GR, HC), ALU.mult).then_inc(s_kd, 1)
                    v.wait_ge(s_kd, kv * 4 + 3)
                    v.tensor_tensor(kvh, kvh, lns[:, 0:2, :].unsqueeze(2).broadcast_to([TN, 2, HEADS, HC]), ALU.mult).then_inc(s_kd, 1)
                    v.wait_ge(s_kd, kv * 4 + 4)
                    v.tensor_tensor(kvh, kvh, lns[:, 2:4, :].unsqueeze(2).broadcast_to([TN, 2, HEADS, HC]), ALU.add).then_inc(s_kvn, 1)
                if mix is not None:
                    v.wait_ge(s_b1, mix * 2 + 4)
                    v.wait_ge(s_mp, fin(mix))
                    v.tensor_tensor(xch[:, u, :, :], xch[:, u, :, :], ps_acc[0:TN, :].rearrange("p (t d) -> p t d", t=2), ALU.add).then_inc(s_bs, 1)

            def between(step):
                if step == 0:
                    v.wait_ge(s_kva, NT + 3)
                    v.wait_ge(s_mask, 1 + P // HC)
                    v.tensor_tensor(kv_t[:, :, :], ps_acc[:, 0:KC * P].rearrange("p (c n) -> p c n", c=KC),
                                    block_mask[:, :].unsqueeze(1).broadcast_to([P, KC, P]), ALU.mult).then_inc(s_c, 1)
                if step == 1:
                    v.wait_ge(s_cp, 1)
                    v.tensor_copy(p_sb[:, :, :], ps_kv[:, :].rearrange("p (c n) -> p c n", c=KC)).then_inc(s_c, 1)
                if step == 2:
                    v.wait_ge(s_cp, 2)
                    v.tensor_tensor(p_sb[:, :, :], ps_xt[:, :].rearrange("p (c n) -> p c n", c=KC), w1_sb[:, :, :], ALU.add).then_inc(s_c, 1)
                    v.tensor_tensor(bm[:, :], ps_acc[:, 0:KC], b1c[:, :], ALU.add).then_inc(s_c, 1)
                    v.tensor_tensor(w2_lo[:, :, :], w2_sb, w2_hi[:, :, :].bitcast(F32), ALU.subtract).then_inc(s_c, 1)
                    v.wait_ge(s_ca, 2)
                    v.wait_ge(s_c, 3)
                    v.tensor_tensor(m_lo[:, :, :], p_sb[:, :, :], m_hi[:, :, :].bitcast(F32), ALU.subtract).then_inc(s_c, 1)

            def start(k):
                for h in range(2):
                    v.wait_ge(s_hot[h], fin(k * NG, 1))
                v.wait_ge(s_seg[1], fin(k * NG, 2))
                v.tensor_scalar(rel[:, :], rel[:, :], -float(W), None, ALU.add).then_inc(s_pass, 1)
                v.tensor_copy(brow[0:1, 0:1], brow[0:1, NG:NG + 1]).then_inc(s_pass, 1)
                v.wait_ge(s_pass, k * 3 - 1)
                v.tensor_scalar(brow[0:1, 1:NG + 1], brow[0:1, 1:NG + 1], W, None, ALU.add).then_inc(s_pass, 1)
                v.wait_ge(s_pass, k * 3)
                v.sem_inc(s_carry, 1)
                take(0, 0)
                first_half(k * NG)

            def first_half(it):
                one_hot(it, 0, 0)
                low_edges(it, 0)

            def epilogue(it):
                flush(it, degrees(it, NG))
                v.wait_ge(s_dacc, fin(it, 1))
                v.wait_ge(s_acc, fin(it, 1))
                v.sem_inc(s_sums, 1)

            first_half(0)
            schedule(v, body, between)
            general(v, body, start, epilogue)

            v.sem_inc(s_r2, 4)
            v.memset(zcol[:, :], 0.0).then_inc(s_nd, 1)
            v.wait_ge(s_np, 1)
            v.tensor_scalar(degs[:, 0, :], ps_t[0:TN, 0:NT], 1.0, None, ALU.max).then_inc(s_nd, 1)
            v.wait_ge(s_na, 1)
            v.reciprocal(degs[:, 2, :], degs[:, 1, :]).then_inc(s_nd, 1)
            v.wait_ge(s_nd, 3)
            v.scalar_tensor_tensor(norm[:, :], ps_t[0:TN, 0:NT], 0.0, degs[:, 2, :], ALU.is_gt, ALU.mult).then_inc(s_nd, 1)
            v.wait_ge(s_nd, 4)

            def rows(c, u, i):
                v.wait_ge(s_fx[u], i + 2)
                v.sem_inc(s_carry, 1)
                for j in range(2):
                    v.bn_stats(st6n[:, j, :], y_n[:, u, j, :]).then_inc(s_fs, 1)
                for j in range(2):
                    v.wait_ge(s_fs, c * 4 + (j + 1))
                    wait_past(v, s_fv, c * 2)
                    v.sem_inc(s_carry, 1)
                    v.bn_aggr(mvn[:, j, :], st6n[:, j, :]).then_inc(s_fs, 1)
                v.wait_ge(s_fs, c * 4 + 4)
                v.wait_ge(s_r2, c * 2 + 2)
                v.tensor_scalar(ven[:, u, :], mvn[:, :, 1], EPS, None, ALU.add).then_inc(s_fv, 1)
                v.tensor_scalar(nmn[:, u, :], mvn[:, :, 0], -1.0, None, ALU.mult).then_inc(s_fv, 1)

            def inverse(c, u):
                v.wait_ge(s_sdn, c + 1)
                v.wait_ge(s_mean, c + 1)
                v.reciprocal(rst[:, u, :], sdn[:, u, :]).then_inc(s_rst, 1)
                v.reciprocal(r2[:, ds(c * 2, 2)], sdn[:, u, :]).then_inc(s_r2, 1)
                v.wait_ge(s_rst, c + 1)
                v.tensor_tensor(nmr2[:, ds(c * 2, 2)], nmn[:, u, :], rst[:, u, :], ALU.mult).then_inc(s_r2, 1)

            def step(c, u, i):
                rows(c, u, i)
                inverse(c, u)

            node_chunks(v, step)
            row = lambda n: rt[0:1, n, :]
            one = lambda n: rs[0:1, n:n + 1]
            v.wait_ge(s_r2, 2 * NC + 4)
            v.tensor_reduce(nsum[:, :], nmr2[:, :], AX, ALU.add).then_inc(s_rd, 1)
            v.wait_ge(s_rp, 1)
            v.tensor_copy(one(0), ps_t[0:1, 0:1]).then_inc(s_rd, 1)
            v.wait_ge(s_rd, 2)
            v.wait_ge(s_mean, NC + 2)
            v.tensor_scalar(mrow[:, :], ps_kv[0:1, 0:D], one(0), 1.0 / N, ALU.add, ALU.mult).then_inc(s_rd, 1)
            v.wait_ge(s_rp, 2)
            v.tensor_copy(mean_c[:, :], ps_y[:, 0:KC]).then_inc(s_rm, 1)
            v.wait_ge(s_rp, 3)
            v.wait_ge(s_rw, 32)
            v.tensor_tensor(row(1), ps_t[0:1, 0:EX], row(0), ALU.add).then_inc(s_rd, 1)
            v.wait_ge(s_rd, 4)
            v.tensor_reduce(one(1), row(1), AX, ALU.max, negate=True).then_inc(s_rd, 1)

            def softmax_rest(exps, total, inverse, result, n, m=EX):
                v.tensor_reduce(total, exps[:, 0:m], AX, ALU.add).then_inc(s_rd, 1)
                v.wait_ge(s_rd, n)
                v.reciprocal(inverse, total).then_inc(s_rd, 1)
                v.wait_ge(s_rd, n + 1)
                v.tensor_scalar(result[:, 0:m], exps[:, 0:m], inverse, None, ALU.mult).then_inc(s_rd, 1)
                v.wait_ge(s_rd, n + 2)

            v.wait_ge(s_ra, 1)
            softmax_rest(row(2), one(2), one(3), row(3), 6)
            v.tensor_scalar(row(4), row(3), float(N), None, ALU.mult).then_inc(s_rd, 1)
            v.wait_ge(s_rd, 9)
            v.tensor_scalar(row(5), row(4), CAPACITY, None, ALU.max).then_inc(s_rd, 1)
            v.wait_ge(s_rd, 10)
            v.reciprocal(row(6), row(5)).then_inc(s_rd, 1)
            v.wait_ge(s_rd, 11)
            v.tensor_scalar(row(6), row(6), CAPACITY, -1.0, ALU.mult, ALU.add).then_inc(s_rd, 1)
            v.wait_ge(s_rd, 12)
            v.scalar_tensor_tensor(row(7), row(4), CAPACITY, row(6), ALU.is_gt, ALU.mult).then_inc(s_rd, 1)
            v.wait_ge(s_rd, 13)
            v.tensor_scalar(row(7), row(7), 1.0, None, ALU.add).then_inc(s_rd, 1)
            v.wait_ge(s_rd, 14)
            v.tensor_tensor(row(8), row(3), row(7), ALU.mult).then_inc(s_rd, 1)
            v.wait_ge(s_rd, 15)
            v.tensor_reduce(one(5), row(8), AX, ALU.max, negate=True).then_inc(s_rd, 1)
            v.wait_ge(s_ra, 2)
            softmax_rest(row(9), one(6), one(7), row(10), 17)
            v.max(row(11), row(10)).then_inc(s_rd, 1)
            v.wait_ge(s_rd, 20)
            v.max_index(top_i[:, :], row(11), row(10)).then_inc(s_top, 1)
            v.tensor_scalar(one(8), rt[0:1, 11, 0:1], -1.0, None, ALU.mult).then_inc(s_rd, 1)
            v.wait_ge(s_ra, 3)
            softmax_rest(row(12), one(9), one(10), row(13), 22, 2)
            v.wait_ge(s_rd, 24)
            v.sem_inc(s_top, 1)

            def rows_lo(c, u, i):
                v.wait_ge(s_xfh, c + 1)
                v.tensor_tensor(xf_lo[:, :, 0:CN], ps_xt[:, 0:KC * CN].rearrange("p (c n) -> p c n", c=KC), xf_hi[:, :, 0:CN].bitcast(F32),
                                ALU.subtract).then_inc(s_xfl, 1)

            def hidden(c, u, i):
                for q in range(FC // 2):
                    v.wait_ge(s_hh, c * (FC // 2) + (q + 1))
                    v.tensor_tensor(h_lo[:, u, 2 * q:2 * q + 2, :], h32[:, 2 * q:2 * q + 2, :], h_hi[:, u, 2 * q:2 * q + 2, :].bitcast(F32),
                                    ALU.subtract).then_inc(s_hl, 1)

            def added(c, u, i):
                v.wait_ge(s_g2[u], i + 1)
                v.wait_ge(s_xlb[u], i + 1)
                wait_past(v, s_rn[u], i * 2)
                v.tensor_tensor(o_sb[:, u, :, :], [ps_kv, ps_acc][u][0:TN, :].rearrange("p (t d) -> p t d", t=2), xlb[:, u, :, :],
                                ALU.add).then_inc(s_od[u], 1)
                v.wait_ge(s_od[u], i + 1)
                v.sem_inc(s_carry, 1)
                for j in range(2):
                    v.bn_stats(st6x[:, j, :], o_sb[:, u, j, :]).then_inc(s_xs, 1)
                for j in range(2):
                    v.wait_ge(s_xs, c * 4 + (j + 1))
                    wait_past(v, s_vx, c * 2)
                    v.sem_inc(s_carry, 1)
                    v.bn_aggr(mvx[:, j, :], st6x[:, j, :]).then_inc(s_xs, 1)
                v.wait_ge(s_xs, c * 4 + 4)
                v.tensor_scalar(vex[:, u, :], mvx[:, :, 1], EPS, None, ALU.add).then_inc(s_vx, 1)
                v.tensor_scalar(nmx[:, u, :], mvx[:, :, 0], -1.0, None, ALU.mult).then_inc(s_vx, 1)

            def finish(c, u, i):
                v.wait_ge(s_rn[u], i * 2 + 2)
                v.tensor_tensor(res[:, u, :, :], res[:, u, :, :], grow[:, :].unsqueeze(1).broadcast_to([TN, 2, D]), ALU.mult).then_inc(s_rg[u], 1)
                v.wait_ge(s_rg[u], i + 1)
                v.wait_ge(s_xb[u], i + 1)
                v.tensor_tensor(res[:, u, :, :], res[:, u, :, :], xb[:, u, :, :], ALU.add).then_inc(s_res[u], 1)

            def step(c, u, i):
                fixed = isinstance(c, int)
                if not (fixed and c + 1 >= NC):
                    hidden(c + 1, 1 - u, i + u)
                if not (fixed and c + 2 >= NC):
                    rows_lo(c + 2, u, i + 1)
                if not (fixed and c == 0):
                    finish(c - 1, 1 - u, i + (u - 1))
                added(c, u, i)

            v.memset(xf_hi[:, :, CN:CW].bitcast(F32), 0.0).then_inc(s_w1l, 1)
            v.memset(xf_lo[:, :, CN:CW].bitcast(F32), 0.0).then_inc(s_w1l, 1)
            rows_lo(0, 0, 0)
            v.wait_ge(s_bp, 1)
            v.tensor_copy(wts[:, :], ps_y[:, 0:2]).then_inc(s_rm, 1)
            for j in range(2):
                v.wait_ge(s_w1h, j + 1)
                v.tensor_tensor(fw1_lo[:, :, j * F:(j + 1) * F], fw1_st[:, j, :, :], fw1_hi[:, :, j * F:(j + 1) * F].bitcast(F32),
                                ALU.subtract).then_inc(s_w1l, 1)
            v.wait_ge(s_rm, 2)
            for j in range(2):
                v.wait_ge(s_fw2[j], 16)
                v.tensor_scalar(fw2_st[:, j, :, :], fw2_st[:, j, :, :], wts[:, j:j + 1], None, ALU.mult).then_inc(s_w2s, 1)
            v.wait_ge(s_fb, 16 * 6)
            for j in range(2):
                v.tensor_scalar(fb2r[0:1, j, :], fb2r[0:1, j, :], wts[0:1, j:j + 1], None, ALU.mult).then_inc(s_w2s, 1)
            for j in range(2):
                v.wait_ge(s_w2h, j + 1)
                v.tensor_tensor(fw2_lo[:, j * (FC // 2):(j + 1) * (FC // 2), :], fw2_st[:, j, :, :],
                                fw2_hi[:, j * (FC // 2):(j + 1) * (FC // 2), :].bitcast(F32), ALU.subtract).then_inc(s_w2l, 1)
            hidden(0, 0, 0)
            rows_lo(1, 1, 0)
            v.wait_ge(s_bp, 2)
            v.tensor_copy(b2w[:, :], ps_acc[0:TN, 0:D]).then_inc(s_b2w, 1)
            chunks(v, step)
            finish(NC - 1, (NC - 1) % 2, NC // 2)


_ARGS = (("x", "x"), ("src_l", None), ("dst_l", None), ("edges", "edge_attr_256"), ("wgnn", "L0_gnn_weights"),
         ("hbias", "L0_gnn_h_bias"), ("w_qkv", "L0_mix_w_qkv"), ("wq_t", None), ("b_qkv", "L0_mix_b_qkv"), ("bq_l", None),
         ("kln_g", "L0_mix_kln_g"), ("kln_b", "L0_mix_kln_b"), ("vln_g", "L0_mix_vln_g"), ("vln_b", "L0_mix_vln_b"),
         ("w1", "L0_mix_w1"), ("b1_l", None), ("w2", "L0_mix_w2"), ("b2", "L0_mix_b2"), ("wr", "L0_ffn_Wr"),
         ("br", "L0_ffn_br"), ("fw1", "L0_ffn_W1"), ("fb1_l", None), ("fw2", "L0_ffn_W2"), ("fb2", "L0_ffn_b2"),
         ("gamma", "L0_ffn_gamma"), ("beta", "L0_ffn_beta"))


def kernel(**inputs):
    import numpy as np
    import concourse.bacc as bacc
    from concourse.bass_utils import run_bass_kernel_spmd

    full = (NG - 1) * GE
    by_group = lambda a: np.asarray(a)[:full].reshape(NG - 1, P, GT).transpose(1, 0, 2).reshape(P, -1)
    dst, src = np.asarray(inputs["dst"]), np.asarray(inputs["src"])
    dst_last, src_last = np.full((P, GT), int(MASKED), dst.dtype), np.zeros((P, GT), src.dtype)
    fresh = E - full
    dst_last[P - fresh:, 0] = dst[full:]
    src_last[:, 0] = src[LAST:]
    dst = np.concatenate([by_group(dst), dst_last], axis=1)
    src = np.concatenate([by_group(src), src_last], axis=1)
    w_qkv = np.asarray(inputs["L0_mix_w_qkv"])
    wq_t = w_qkv.reshape(D, HEADS, 3, HC)[:, :, 0, :].reshape(D, D).T
    bq_l = np.asarray(inputs["L0_mix_b_qkv"]).reshape(HEADS, 3, HC)[:, 0, :].reshape(KC, P).T
    laid = {"src_l": src, "dst_l": dst, "wq_t": wq_t, "bq_l": bq_l,
            "b1_l": np.asarray(inputs["L0_mix_b1"]).reshape(KC, P).T,
            "fb1_l": np.asarray(inputs["L0_ffn_b1"]).reshape(EX, F // P, P).transpose(0, 2, 1)}

    nc = bacc.Bacc("TRN2", target_bir_lowering=False, num_devices=1)
    arrays, args = {}, []
    for name, source in _ARGS:
        a = np.ascontiguousarray(laid[name] if source is None else np.asarray(inputs[source]))
        arrays[name] = a
        args.append(nc.dram_tensor(name, a.shape, mybir.dt.from_np(a.dtype), kind="ExternalInput").ap())
    out = nc.dram_tensor("out", (N, D), F32, kind="ExternalOutput").ap()
    gps_layer(nc, *args, out)
    r = run_bass_kernel_spmd(nc, [arrays], core_ids=[0])
    return r.results[0]["out"]
```
